# Optimizing a Trainium2 kernel written in Bass

```python
import numpy as np
import jax
import jax.numpy as jnp

def _softmax(x, axis=-1):
    return jax.nn.softmax(x, axis=axis)

def _gelu(x):
    return jax.nn.gelu(x, approximate=True)

def _silu(x):
    return jax.nn.silu(x)

def _sigmoid(x):
    return jax.nn.sigmoid(x)

def _layernorm(x, axis=-1, eps=1e-05):
    m = jnp.mean(x, axis=axis, keepdims=True)
    v = jnp.var(x, axis=axis, keepdims=True)
    return (x - m) / jnp.sqrt(v + eps)

def _scatter_add(tgt, idx, src, axis=0):
    return tgt.at[idx].add(src)

def _segment_sum(src, seg, n):
    return jax.ops.segment_sum(src, seg, n)
kernel_name = 'mk_seq_preln_d1_jaxref_r8_246a9d'

def setup_inputs(seed: int=0):
    np.random.seed(seed)
    _w = jnp.asarray

    def _L0_attn_setup():
        import jax, jax.numpy as jnp
        import numpy as np
        import math
        N_HEAD = 16
        N_EMBD = 256
        key = jax.random.key(seed)
        k1, k2, k3, k4, k5 = jax.random.split(key, 5)
        B, T, C = (4, 256, N_EMBD)
        x = jax.random.normal(k1, (B, T, C), dtype=jnp.float32)
        s_attn = 1.0 / math.sqrt(C)
        w_attn = jax.random.normal(k2, (C, 3 * C), dtype=jnp.float32) * s_attn
        b_attn = jnp.zeros((3 * C,), dtype=jnp.float32)
        w_proj = jax.random.normal(k3, (C, C), dtype=jnp.float32) * s_attn
        b_proj = jnp.zeros((C,), dtype=jnp.float32)
        return {'x': x, 'w_attn': w_attn, 'b_attn': b_attn, 'w_proj': w_proj, 'b_proj': b_proj}
    _L0_attn_in = _L0_attn_setup()

    def _L0_ffn_setup():
        import jax, jax.numpy as jnp
        import numpy as np
        B, S, D = (1, 128, 256)
        E, K, F = (64, 8, 96)
        C = 32

        def _moe(x, router_w, w1, v1, w2):
            T = x.shape[0]
            logits = x @ router_w.T
            probs = jax.nn.softmax(logits, axis=-1)
            wts, idx = jax.lax.top_k(probs, K)
            wts = wts / jnp.sum(wts, axis=-1, keepdims=True)
            R = T * K
            e_flat = idx.reshape(-1)
            tok = jnp.arange(R) // K
            order = jnp.argsort(e_flat)
            e_s, tok_s = (e_flat[order], tok[order])
            w_s = wts.reshape(-1)[order]
            counts = jnp.bincount(e_flat, length=E)
            starts = jnp.cumsum(counts) - counts
            pos = jnp.arange(R) - starts[e_s]
            valid = pos < C
            pos_c = jnp.minimum(pos, C - 1)
            xg = jnp.zeros((E, C, D), x.dtype).at[e_s, pos_c].add(jnp.where(valid[:, None], x[tok_s], 0.0))
            h = jax.nn.silu(jnp.einsum('ecd,efd->ecf', xg, w1)) * jnp.einsum('ecd,efd->ecf', xg, v1)
            y = jnp.einsum('ecf,efd->ecd', h, w2)
            yr = y[e_s, pos_c] * jnp.where(valid, w_s, 0.0)[:, None]
            return jnp.zeros((T, D), x.dtype).at[tok_s].add(yr)
        key = jax.random.key(seed)
        k0, k1, k2, k3, k4 = jax.random.split(key, 5)
        return {'hidden_states': jax.random.normal(k0, (B, S, D), jnp.float32), 'router_w': jax.random.normal(k1, (E, D), jnp.float32) * 0.02, 'w1': jax.random.normal(k2, (E, F, D), jnp.float32) * 0.02, 'v1': jax.random.normal(k3, (E, F, D), jnp.float32) * 0.02, 'w2': jax.random.normal(k4, (E, F, D), jnp.float32) * 0.02}
    _L0_ffn_in = _L0_ffn_setup()
    _d = {'L0_attn_x': _L0_attn_in['x'], 'L0_attn_w_attn': _L0_attn_in['w_attn'], 'L0_attn_b_attn': _L0_attn_in['b_attn'], 'L0_attn_w_proj': _L0_attn_in['w_proj'], 'L0_attn_b_proj': _L0_attn_in['b_proj'], 'L0_ffn_router_w': _L0_ffn_in['router_w'], 'L0_ffn_w1': _L0_ffn_in['w1'], 'L0_ffn_v1': _L0_ffn_in['v1'], 'L0_ffn_w2': _L0_ffn_in['w2']}
    _x0 = _d['L0_attn_x']
    _d['L0_attn_x'] = jax.random.normal(jax.random.fold_in(jax.random.key(seed), 1), (4, 256, 256), dtype=_x0.dtype)
    del _x0
    return _d

def reference(L0_attn_x, L0_attn_w_attn, L0_attn_b_attn, L0_attn_w_proj, L0_attn_b_proj, L0_ffn_router_w, L0_ffn_w1, L0_ffn_v1, L0_ffn_w2):

    def _L0_attn_ref(x, w_attn, b_attn, w_proj, b_proj):
        import jax, jax.numpy as jnp
        import numpy as np
        import math
        N_HEAD = 16
        N_EMBD = 256
        B, T, C = x.shape
        H = N_HEAD
        D = C // H
        qkv = x @ w_attn + b_attn
        q, k, v = jnp.split(qkv, 3, axis=2)
        q = q.reshape(B, T, H, D).transpose(0, 2, 1, 3)
        k = k.reshape(B, T, H, D).transpose(0, 2, 1, 3)
        v = v.reshape(B, T, H, D).transpose(0, 2, 1, 3)
        scale = 1.0 / math.sqrt(D)
        att = jnp.einsum('bhqd,bhkd->bhqk', q, k) * scale
        causal = jnp.tril(jnp.ones((T, T), dtype=bool))
        att = jnp.where(causal[None, None], att, -jnp.inf)
        att = jax.nn.softmax(att.astype(jnp.float32), axis=-1).astype(att.dtype)
        y = jnp.einsum('bhqk,bhkd->bhqd', att, v)
        y = y.transpose(0, 2, 1, 3).reshape(B, T, C)
        return y @ w_proj + b_proj

    def _L0_ffn_ref(hidden_states, router_w, w1, v1, w2):
        import jax, jax.numpy as jnp
        import numpy as np
        B, S, D = (1, 128, 256)
        E, K, F = (64, 8, 96)
        C = 32

        def _moe(x, router_w, w1, v1, w2):
            T = x.shape[0]
            logits = x @ router_w.T
            probs = jax.nn.softmax(logits, axis=-1)
            wts, idx = jax.lax.top_k(probs, K)
            wts = wts / jnp.sum(wts, axis=-1, keepdims=True)
            R = T * K
            e_flat = idx.reshape(-1)
            tok = jnp.arange(R) // K
            order = jnp.argsort(e_flat)
            e_s, tok_s = (e_flat[order], tok[order])
            w_s = wts.reshape(-1)[order]
            counts = jnp.bincount(e_flat, length=E)
            starts = jnp.cumsum(counts) - counts
            pos = jnp.arange(R) - starts[e_s]
            valid = pos < C
            pos_c = jnp.minimum(pos, C - 1)
            xg = jnp.zeros((E, C, D), x.dtype).at[e_s, pos_c].add(jnp.where(valid[:, None], x[tok_s], 0.0))
            h = jax.nn.silu(jnp.einsum('ecd,efd->ecf', xg, w1)) * jnp.einsum('ecd,efd->ecf', xg, v1)
            y = jnp.einsum('ecf,efd->ecd', h, w2)
            yr = y[e_s, pos_c] * jnp.where(valid, w_s, 0.0)[:, None]
            return jnp.zeros((T, D), x.dtype).at[tok_s].add(yr)
        b, s, d = hidden_states.shape
        x = hidden_states.transpose(1, 0, 2).reshape(s * b, d)
        out = _moe(x, router_w, w1, v1, w2)
        return out.reshape(s, b, d).transpose(1, 0, 2)
    x = L0_attn_x
    x = x + _L0_attn_ref(_layernorm(x, axis=-1), L0_attn_w_attn, L0_attn_b_attn, L0_attn_w_proj, L0_attn_b_proj)
    x = x + _L0_ffn_ref(_layernorm(x, axis=-1), L0_ffn_router_w, L0_ffn_w1, L0_ffn_v1, L0_ffn_w2)
    return x

_drawn_inputs = setup_inputs


def setup_inputs(seed=0):
    import zlib

    import numpy as np

    out = dict(_drawn_inputs(seed))
    spreads = {'L0_attn_b_attn': (0.0, 0.1), 'L0_attn_b_proj': (0.0, 0.1)}
    factors = {'L0_ffn_router_w': 8.0, 'L0_ffn_w1': 8.0, 'L0_ffn_v1': 8.0, 'L0_ffn_w2': 8.0}
    for name, (base, spread) in spreads.items():
        noise = np.random.default_rng([zlib.crc32(name.encode()), seed]).standard_normal(out[name].shape)
        drawn = base * np.exp(spread * noise) if base else spread * noise
        out[name] = jnp.asarray(drawn.astype(out[name].dtype))
    for name, factor in factors.items():
        out[name] = (out[name] * factor).astype(out[name].dtype)
    return out
```

```python
from contextlib import ExitStack

import concourse.bass as bass
from concourse import mybir

F32 = mybir.dt.float32
BF16 = mybir.dt.bfloat16
F16 = mybir.dt.float16
U32 = mybir.dt.uint32
ALU = mybir.AluOpType
ACT = mybir.ActivationFunctionType
AX = mybir.AxisListType

P = 128
B, T, C = 4, 256, 256
H, D = 16, 16
E, TOPK, F, CAP = 64, 8, 96, 32
KC = C // P
HT = T // P
NT = B * HT
HG = 8
NU = B * H // HG
PARTS = [(0, 0), (0, 1), (1, 0), (1, 1), (0, 2), (2, 0)]
KP = D * len(PARTS)
EPS = 1e-5
SCALE = D ** -0.5
MASKED = -1e30
EG = P // CAP
NG = E // EG
ROW = C + E
NTOK = B * T
W2S = 9
PIECES = 6
STP = 3
LAST_STEP = 2 * (B - 1) + 8
N_PACK = 1 + len(PARTS) + sum(pq > pk for pq, pk in PARTS)
ATTN_CONSTS = 6
MOE_CONSTS = 5
SPREAD = [2, 3, 0]


def misc_schedule():
    use = {}
    for s in range(LAST_STEP + 1):
        for b in range(B):
            if s == 2 * b + 7:
                use["logits", b] = len(use)
        if 1 <= s <= NU:
            use["negmax", s - 1] = len(use)
        for b in range(B):
            if s == 2 * b + 5:
                use["proj", b] = len(use)
        for b in range(B):
            if s == 2 * b + 6:
                use["xt", b] = len(use)
    return use


def build(nc, x, wqk, bqk, wv, bv, wproj, bproj, rwt, w13, w2, out):
    with ExitStack() as ctx:
        ent = ctx.enter_context

        def sb(name, shape, dt):
            return ent(nc.sbuf_tensor(name, shape, dt))

        def sem(name):
            return ent(nc.semaphore(name))

        x_sb = sb("x_sb", [P, NT, C], F32)
        rows = sb("rows", [P, NT, ROW], F32)
        id32 = sb("id32", [P, P], F32)
        id16 = sb("id16", [P, P], BF16)
        causal = sb("causal", [P, P], BF16)
        before = sb("before", [P, 7, P], BF16)
        ones = sb("ones", [P, 4 * P], BF16)
        spread = sb("spread", [E, NG, P], BF16)
        tokid = sb("tokid", [P, NTOK], F16)
        w_proj = sb("w_proj", [P, KC, C], F32)
        w_rt = sb("w_rt", [P, KC, E], F32)
        b_v = sb("b_v", [P, C], F32)
        b_proj = sb("b_proj", [P, C], F32)
        b_qk = sb("b_qk", [P, 4], F32)
        stats = sb("stats", [P, 2, HT, 6], F32)
        mv = sb("mv", [P, 2, HT, 2], F32)
        ve = sb("ve", [P, 2, HT], F32)
        rstd = sb("rstd", [P, 2, HT], F32)
        mhalf = sb("mhalf", [P, HT], F32)
        sel = sb("sel", [P, NT, E], BF16)
        slot_c = sb("slot_c", [P, 2], F32)
        pc = sb("pc", [P, EG], F32)
        eq4 = sb("eq4", [P, EG], F32)
        tok_n = sb("tok_n", [P, NG], F32)
        tok_i = sb("tok_i", [P, NG], U32)
        oz = sb("oz", [P, 2, 32], F32)
        m8 = sb("m8", [P, NT, 8], F32)
        negm = sb("negm", [P, HT], F32)
        wsum = sb("wsum", [P, HT], F32)
        wrec = sb("wrec", [P, HT], F32)
        lg = sb("lg", [P, HT, E], F32)
        lr = sb("lr", [P, HT, E], F32)
        ee = sb("ee", [P, HT, E], F32)
        nm = sb("nm", [P, 2, HT, HG], F32)
        nmp = sb("nmp", [P, 2, HT, 2, HG], BF16)
        nmt = sb("nmt", [2 * HG, 2, T], BF16)
        y_t = sb("y_t", [P, 2, KC, T], F32)
        rden = sb("rden", [P, T], F32)
        xt2 = sb("xt2", [P, KC, T], F32)

        size = {F32: 4, BF16: 2, F16: 2}
        at = [(nc.sbuf_base + 31) // 32 * 32]
        words = (nc.sbuf_bytes_remaining - 256) // 4
        top = at[0] + 4 * words - 64
        sb("arena", [P, words], F32)

        def place(name, shape, dt, offset=None):
            n = size[dt]
            for d in shape[1:]:
                n *= d
            n = (n + 31) // 32 * 32
            if offset is None:
                offset = at[0]
                at[0] += n
                assert at[0] <= top, (name, at[0], top)
            return nc.alloc_sbuf_tensor_at(name, shape, dt, offset=offset)

        W13B, W2B = EG * KC * 2 * F * 4, EG * C * 4
        w13_at, w2_at = {}, {}
        pack, pack_at = [], []
        for b in range(B):
            pack_at.append(at[0])
            pack.append(place(f"pack{b}", [KP + 2, HG, 2, 2, T], BF16))
            w13_at[8 + 2 * b] = pack_at[b]
            w13_at[9 + 2 * b] = pack_at[b] + W13B
            w2_at[1 + b] = pack_at[b] + 2 * W13B
        vz_at = at[0]
        vz = place("vz", [P, NT, H, 32], F32)
        for n in range(4):
            w2_at[5 + n] = vz_at + n * W2B
        pt_at = at[0]
        pt = place("pt", [P, 2 * STP, 1024], F32)
        a_at = at[0]
        w_qk = place("w_qk", [P, KC, 2 * C], F32)
        w_v = place("w_v", [P, KC, C], F32)
        xn = place("xn", [P, 2, HT, C], F32)
        xnt = place("xnt", [P, 2, KC, T], F32)
        spl = place("spl", [P, 2, 3 * 2, 2 * T], BF16)
        res = place("res", [P, 2, 4, T], F32)
        a_end = at[0]
        free_chunks = min(3, (top - a_end) // W13B)
        assert a_at + 5 * W13B + W2B <= a_end
        for n in range(5):
            w13_at[free_chunks + n] = a_at + n * W13B
        w2_at[0] = a_at + 5 * W13B
        for n in range(free_chunks):
            w13_at[n] = a_end + n * W13B
        assert free_chunks == 3
        w13_sb = [nc.alloc_sbuf_tensor_at(f"w13_{g}", [P, EG, KC, 2 * F], F32, offset=w13_at[g]) for g in range(NG)]
        w2_sb = [nc.alloc_sbuf_tensor_at(f"w2_{g}", [F, EG, C], F32, offset=w2_at[g]) for g in range(W2S)]
        d_at = at[0]
        at[0] = pt_at
        cumc = place("cumc", [E, NTOK], BF16)
        junk = place("junk", [P, 2, NTOK], BF16)
        grow = place("grow", [P, 4, ROW], F32)
        xgt = place("xgt", [P, 2, KC, P], F32)
        sil = place("sil", [P, F], F32)
        hh = place("hh", [P, F], F32)
        ht = place("ht", [F, 2, P], F32)
        y3 = place("y3", [P, 2, 3, C], BF16)
        yr = place("yr", [P, C], F32)
        g4 = place("g4", [P, EG], F32)
        gate = place("gate", [P, NG], F32)
        assert at[0] <= a_at
        onehot = junk
        at[0] = d_at

        xrow = nc.dram_tensor("xrow", [NTOK, ROW], F32, kind="Internal").ap()

        ps = [ent(nc.psum_tensor(f"pair{n}", [P, 1024], F32)) for n in range(4)]

        def bank(n):
            return ps[n // 2][:, (n % 2) * 512:(n % 2) * 512 + 512]

        x_in = [sem(f"x_in{b}") for b in range(B)]
        wqk_in, wv_in, bqk_in, small_in = sem("wqk_in"), sem("wv_in"), sem("bqk_in"), sem("small_in")
        scaled = sem("scaled")
        ones_ready, slotc_ready = sem("ones_ready"), sem("slotc_ready")
        zeroed, id_ready, attn_const, moe_const = sem("zeroed"), sem("id_ready"), sem("attn_const"), sem("moe_const")
        var_ready, rstd_ready, xn_ready = sem("var_ready"), sem("rstd_ready"), sem("xn_ready")
        xt_ps, xt_ready = sem("xt_ps"), sem("xt_ready")
        qk_ps, v_ps = sem("qk_ps"), sem("v_ps")
        h_ready, r_ready, m_ready, l_ready, v_ready = (sem("h_ready"), sem("r_ready"), sem("m_ready"),
                                                       sem("l_ready"), sem("v_ready"))
        packed = [sem(f"packed{b}") for b in range(B)]
        xb_ready = sem("xb_ready")
        s_ps, max_done = sem("s_ps"), sem("max_done")
        nmp_ready = sem("nmp_ready")
        negrow_in = [sem(f"negrow_in{n}") for n in range(2)]
        st_ps, exp_done, causal_done = sem("st_ps"), sem("exp_done"), sem("causal_done")
        pv_ps, yt_ready = sem("pv_ps"), sem("yt_ready")
        misc_ps, misc_free = sem("misc_ps"), sem("misc_free")
        var2_ready, rstd2_ready, xn2_ready = sem("var2_ready"), sem("rstd2_ready"), sem("xn2_ready")
        negm_ready, e_ready, sel_ready, rows_ready = (sem("negm_ready"), sem("e_ready"), sem("sel_ready"),
                                                      sem("rows_ready"))
        rows_out = [sem(f"rows_out{b}") for b in range(B)]
        cum_ps, cumc_ready = sem("cum_ps"), sem("cumc_ready")
        spread_ps, count_dve, count_act, tok_ready = (sem("spread_ps"), sem("count_dve"), sem("count_act"),
                                                      sem("tok_ready"))
        row_in = [sem(f"row_in{n}") for n in range(4)]
        w13_in = [sem(f"w13_in{g}") for g in range(NG)]
        w2_in = [sem(f"w2_in{g}") for g in range(NG)]
        xg_ps, xg_ready, gate_ready = sem("xg_ps"), sem("xg_ready"), sem("gate_ready")
        up_ps, sil_ready, hh_ready = sem("up_ps"), sem("sil_ready"), sem("hh_ready")
        ht_ps, ht_ready, down_ps = sem("ht_ps"), sem("ht_ready"), sem("down_ps")
        yh_ready, yr_ready, ym_ready, yl_ready = sem("yh_ready"), sem("yr_ready"), sem("ym_ready"), sem("yl_ready")
        hot_ready, comb_ps, fin_ready, out_done = sem("hot_ready"), sem("comb_ps"), sem("fin_ready"), sem("out_done")
        dve_step = sem("dve_step")
        pool_step = sem("pool_step")

        MISC = misc_schedule()
        misc = bank(7)
        N_SMALL = 4 * 16
        q_of = lambda b, g, h, lo, hi, k: pack[b][0:k, h, 0, g, lo:hi]
        k_of = lambda b, g, h, lo, hi, k: pack[b][0:k, h, 1, g, lo:hi]

        block = ent(nc.Block())

        @block.sync
        def _(sp):
            def load_w13(g):
                sp.dma_start(w13_sb[g][:, :, :, :], w13[g]).then_inc(w13_in[g], 16)

            def load_w2(g):
                sp.dma_start(w2_sb[g % W2S][:, :, :], w2[g]).then_inc(w2_in[g], 16)

            def load_x(b):
                sp.dma_start(x_sb[:, b::B, :], x[b].rearrange("(h p) c -> p h c", p=P)).then_inc(x_in[b], 16)

            load_x(0)
            sp.dma_start(w_qk[:, :, :], wqk.rearrange("(k p) n -> p k n", p=P)).then_inc(wqk_in, 16)
            sp.dma_start(b_qk[:, :], bqk).then_inc(bqk_in, 16)
            load_x(1)
            sp.dma_start(w_v[:, :, :], wv.rearrange("(k p) n -> p k n", p=P)).then_inc(wv_in, 16)
            sp.dma_start(b_v[:, :], bv.partition_broadcast(P)).then_inc(small_in, 16)
            sp.dma_start(b_proj[:, :], bproj.partition_broadcast(P)).then_inc(small_in, 16)
            load_x(2)
            load_x(3)
            sp.dma_start(w_proj[:, :, :], wproj.rearrange("(k p) n -> p k n", p=P)).then_inc(small_in, 16)
            sp.dma_start(w_rt[:, :, :], rwt.rearrange("(k p) n -> p k n", p=P)).then_inc(small_in, 16)
            sp.wait_ge(ones_ready, 1)
            for b in range(B):
                sp.dma_start(pack[b][KP:KP + 2, :, 1, :, :].rearrange("r h g t -> r h (g t)"),
                             ones[0:2 * HG, :]).then_inc(packed[b], 16)
            for b in range(B):
                pair = spl[:, b % 2, :, :]
                for n, (pq, pk) in enumerate(PARTS):
                    if n == 0:
                        sp.wait_ge(h_ready, 4 * (b + 1))
                    if n == 1:
                        sp.wait_ge(m_ready, b + 1)
                    if n == 4:
                        sp.wait_ge(l_ready, b + 1)
                    dst = pack[b][n * D:(n + 1) * D, :, :, :, :]
                    iq, ik = 2 * pq, 2 * pk + 1
                    if ik > iq:
                        sp.dma_start(dst.rearrange("d h a g t -> d h (a g t)"),
                                     pair[:, iq:ik + 1:ik - iq, :]).then_inc(packed[b], 16)
                    else:
                        sp.dma_start(dst[:, :, 0, :, :].rearrange("d h g t -> d h (g t)"),
                                     pair[:, iq, :]).then_inc(packed[b], 16)
                        sp.dma_start(dst[:, :, 1, :, :].rearrange("d h g t -> d h (g t)"),
                                     pair[:, ik, :]).then_inc(packed[b], 16)
                if b < 3:
                    load_w13(b)
            for b in range(B):
                sp.wait_ge(packed[b], 16 * N_PACK)
            sp.wait_ge(l_ready, B)
            sp.wait_ge(v_ready, 4 * B)
            late = list(range(3, 8))
            for s in range(1, LAST_STEP + 2):
                if s <= NU:
                    u = s - 1
                    sp.wait_ge(misc_free, MISC["negmax", u] + 1)
                    sp.dma_start(pack[u // 2][KP:KP + 2, :, 0, u % 2, :], nmt[:, u % 2, :])\
                      .then_inc(negrow_in[u % 2], 16)
                if late:
                    load_w13(late.pop(0))
                    if not late:
                        load_w2(0)
                for b in range(B):
                    if s == 2 * b + 4:
                        sp.wait_ge(st_ps, STP * (2 * b + 2))
                        load_w13(8 + 2 * b)
                        load_w13(9 + 2 * b)
                        load_w2(1 + b)
                    if s == 2 * b + 9:
                        sp.wait_ge(rows_ready, b + 1)
                        sp.dma_start(xrow.rearrange("(h s b) c -> b s h c", b=B, h=HT)[b],
                                     rows[:, b::B, :]).then_inc(rows_out[b], 16)
                if s == LAST_STEP:
                    sp.wait_ge(pv_ps, NU)
                    for n in range(5, W2S):
                        load_w2(n)
            for g in range(W2S, NG):
                sp.wait_ge(down_ps, g - W2S + 1)
                load_w2(g)
            for n in range(B):
                sp.wait_ge(fin_ready, n + 1)
                for t in range(2 * n, 2 * n + 2):
                    b, half = t % B, t // B
                    sp.dma_start(out[b, half * P:(half + 1) * P, :], x_sb[:, t, :]).then_inc(out_done, 16)
            sp.wait_ge(out_done, 16 * NT)

        @block.gpsimd
        def _(pool):
            steps = [0]

            def link(ins):
                steps[0] += 1
                ins.then_inc(pool_step, 1)
                pool.wait_ge(pool_step, steps[0])

            link(pool.memset(id32[:, :], 0.0))
            pool.affine_select(out=id32[:, :], in_=id32[:, :], compare_op=ALU.not_equal, fill=1.0, base=0,
                               pattern=[[-1, P]], channel_multiplier=1).then_inc(id_ready, 1)
            link(pool.memset(mhalf[:, :], -0.5))

            def pow_rstd(n, buf, ready, done):
                pool.wait_ge(ready, n + 1)
                pool.tensor_tensor(out=rstd[:, buf, :], in0=ve[:, buf, :], in1=mhalf[:, :],
                                   op=ALU.pow).then_inc(done, 1)

            pool.memset(ones[:, :], 1.0).then_inc(ones_ready, 1)
            pow_rstd(0, 0, var_ready, rstd_ready)
            pow_rstd(1, 1, var_ready, rstd_ready)
            pool.memset(vz[:, :, :, :], 0.0).then_inc(zeroed, 1)
            for b in range(B):
                if b + 2 < B:
                    pow_rstd(b + 2, b % 2, var_ready, rstd_ready)
                if b == 0:
                    link(pool.memset(id16[:, :], 0.0))
                    pool.affine_select(out=id16[:, :], in_=id16[:, :], compare_op=ALU.not_equal, fill=1.0, base=0,
                                       pattern=[[-1, P]], channel_multiplier=1).then_inc(attn_const, 1)
                    link(pool.memset(causal[:, :], 0.0))
                    pool.affine_select(out=causal[:, :], in_=causal[:, :], compare_op=ALU.is_ge, fill=MASKED, base=0,
                                       pattern=[[-1, P]], channel_multiplier=1).then_inc(attn_const, 1)
                    for par in range(2):
                        pool.memset(oz[:, par, 16 * par:16 * par + 16], 1.0).then_inc(attn_const, 1)
                        pool.memset(oz[:, par, 16 * (1 - par):16 * (1 - par) + 16], 0.0).then_inc(attn_const, 1)
                pool.wait_ge(m_ready, b + 1)
                if b >= 2:
                    pool.wait_ge(packed[b - 2], 16 * N_PACK)
                pool.tensor_tensor(out=spl[:, b % 2, 4:6, :].rearrange("p a n -> p (a n)"),
                                   in0=res[:, b % 2, :, :].rearrange("p m t -> p (m t)"),
                                   in1=spl[:, b % 2, 2:4, :].rearrange("p a n -> p (a n)"),
                                   op=ALU.subtract).then_inc(l_ready, 1)
                pool.wait_ge(xn_ready, HT * (b + 1))
                if b == 0:
                    pool.wait_ge(small_in, N_SMALL)
                for t in range(HT):
                    pool.tensor_tensor(out=x_sb[:, t * B + b, :], in0=x_sb[:, t * B + b, :], in1=b_proj[:, :],
                                       op=ALU.add).then_inc(xb_ready, 1)
            link(pool.memset(before[:, :, :], 1.0))
            pool.affine_select(out=before[:, 0:3, :], in_=before[:, 0:3, :], compare_op=ALU.is_gt, fill=0.0, base=0,
                               pattern=[[0, 3], [1, P]], channel_multiplier=-1).then_inc(moe_const, 1)
            pool.affine_select(out=before[:, 3:7, :], in_=before[:, 3:7, :], compare_op=ALU.is_ge, fill=0.0, base=0,
                               pattern=[[0, 4], [1, P]], channel_multiplier=-1).then_inc(moe_const, 1)

            def causal_zero(n):
                pool.wait_ge(exp_done, n + 1)
                buf, j = n % (2 * STP), n % STP
                v = pt[:, buf, :].rearrange("p (h t) -> p h t", t=T if j < 2 else P)[:, :, 0:P]
                pool.affine_select(out=v, in_=v, compare_op=ALU.is_ge, fill=0.0, base=0,
                                   pattern=[[0, 4 if j < 2 else 8], [1, P]], channel_multiplier=-1)\
                    .then_inc(causal_done, 1)

            def moe_consts(part):
                if part == 0:
                    link(pool.memset(spread[:, :, :], 0.0))
                    pool.affine_select(out=spread[:, :, :].rearrange("e g (q c) -> e g q c", q=EG),
                                       in_=spread[:, :, :].rearrange("e g (q c) -> e g q c", q=EG),
                                       compare_op=ALU.not_equal, fill=1.0, base=0,
                                       pattern=[[-EG, NG], [-1, EG], [0, CAP]], channel_multiplier=1)\
                        .then_inc(moe_const, 1)
                elif part == 1:
                    pool.iota(tokid[:, :].rearrange("p (h b s) -> p h b s", h=HT, b=B),
                              pattern=[[P * B, HT], [1, B], [B, P]], base=0, channel_multiplier=0,
                              allow_small_or_imprecise_dtypes=True).then_inc(moe_const, 1)
                elif part == 2:
                    link(pool.memset(eq4[:, :], 1.0))
                    link(pool.affine_select(out=eq4[:, :], in_=eq4[:, :], compare_op=ALU.is_ge, fill=0.0, base=0,
                                            pattern=[[-CAP, EG]], channel_multiplier=1))
                    link(pool.affine_select(out=eq4[:, :], in_=eq4[:, :], compare_op=ALU.is_ge, fill=0.0,
                                            base=CAP - 1, pattern=[[CAP, EG]], channel_multiplier=-1))
                    link(pool.iota(pc[:, :], pattern=[[-CAP, EG]], base=0, channel_multiplier=1,
                                   allow_small_or_imprecise_dtypes=True))
                    pool.tensor_tensor(out=pc[:, :], in0=pc[:, :], in1=eq4[:, :], op=ALU.mult)\
                        .then_inc(moe_const, 1)

            for s in range(LAST_STEP + 1):
                if 2 <= s < NU + 2:
                    for j in range(STP):
                        causal_zero(STP * (s - 2) + j)
                if s < 3:
                    moe_consts(s)
                for b in range(B):
                    if s == 2 * b + 5:
                        pow_rstd(b, b % 2, var2_ready, rstd2_ready)

            def gather(g):
                if g % 4 == 0:
                    pool.wait_ge(tok_ready, g // 4 + 1)
                if g == 0:
                    for b in range(B):
                        pool.wait_ge(rows_out[b], 16)
                if g >= 4:
                    pool.wait_ge(xg_ps, g - 3)
                    pool.wait_ge(gate_ready, g - 3)
                pool.indirect_dma_start(out=grow[:, g % 4, :], out_offset=None, in_=xrow,
                                        in_offset=bass.IndirectOffsetOnAxis(ap=tok_i[:, g:g + 1], axis=0))\
                    .then_inc(row_in[g % 4], 16)

            for g in range(NG):
                gather(g)

        @block.scalar
        def _(act):
            def copy_xt(b):
                act.wait_ge(xt_ps, b + 1)
                if b >= 2:
                    act.wait_ge(v_ps, b - 1)
                act.activation(xnt[:, b % 2, :, :].rearrange("p k t -> p (k t)"), bank(b % 2),
                               ACT.Copy).then_inc(xt_ready, 1)

            copy_xt(0)
            act.wait_ge(scaled, 2)
            for b in range(B):
                act.wait_ge(qk_ps, b + 1)
                if b >= 2:
                    act.wait_ge(packed[b - 2], 16 * N_PACK)
                for m in range(4):
                    act.activation(spl[:, b % 2, m // 2, (m % 2) * T:(m % 2 + 1) * T],
                                   ps[1 + b % 2][:, m * T:(m + 1) * T], ACT.Identity,
                                   bias=b_qk[:, m:m + 1]).then_inc(h_ready, 1)
                if b + 1 < B:
                    copy_xt(b + 1)
                act.wait_ge(r_ready, 4 * (b + 1))
                act.activation(spl[:, b % 2, 2:4, :].rearrange("p a n -> p (a n)"),
                               res[:, b % 2, :, :].rearrange("p m t -> p (m t)"), ACT.Copy).then_inc(m_ready, 1)

            def exp_piece(n):
                act.wait_ge(st_ps, n + 1)
                if n >= 2 * STP:
                    act.wait_ge(pv_ps, n // STP - 1)
                act.activation(pt[:, n % (2 * STP), :], ps[1 + n % 2][:, :], ACT.Exp).then_inc(exp_done, 1)

            for s in range(LAST_STEP + 1):
                for b in range(B):
                    if s == 2 * b + 8:
                        act.wait_ge(negm_ready, b + 1)
                        for t in range(HT):
                            act.activation(ee[:, t, :], lg[:, t, :], ACT.Exp,
                                           bias=negm[:, t:t + 1]).then_inc(e_ready, 1)
                for b in range(B):
                    if s == 2 * b + 7:
                        act.wait_ge(misc_ps, MISC["logits", b] + 1)
                        if b:
                            act.wait_ge(sel_ready, b)
                            act.wait_ge(e_ready, HT * b)
                        act.activation(lg[:, :, :].rearrange("p t e -> p (t e)"), misc[:, 0:HT * E],
                                       ACT.Copy).then_inc(misc_free, 1)
                if 2 <= s < NU + 2:
                    exp_piece(STP * (s - 2))
                if 1 <= s <= NU:
                    u = s - 1
                    act.wait_ge(misc_ps, MISC["negmax", u] + 1)
                    if u >= 2:
                        act.wait_ge(negrow_in[u % 2], 16 * (u // 2))
                    act.activation(nmt[:, u % 2, :], misc[0:2 * HG, 0:P].bitcast(BF16), ACT.Copy)\
                        .then_inc(misc_free, 1)
                if 2 <= s < NU + 2:
                    exp_piece(STP * (s - 2) + 1)
                    exp_piece(STP * (s - 2) + 2)
                for b in range(B):
                    if s == 2 * b + 6:
                        act.wait_ge(misc_ps, MISC["xt", b] + 1)
                        act.activation(xt2[:, :, :].rearrange("p k t -> p (k t)"), misc[:, :],
                                       ACT.Copy).then_inc(misc_free, 1)

            act.wait_ge(slotc_ready, 1)
            for g in range(1, NG, 2):
                act.wait_ge(spread_ps, g + 1)
                if g > 1:
                    act.wait_ge(count_act, g // 2)
                act.activation(junk[:, 1, :], ps[SPREAD[g % 3]][:, :], ACT.Sign, bias=slot_c[:, 1:2], scale=-1.0,
                               accum_out=tok_n[:, g:g + 1]).then_inc(count_act, 1)

            for g in range(NG):
                act.wait_ge(up_ps, g + 1)
                if g:
                    act.wait_ge(hh_ready, g)
                act.activation(sil[:, :], bank(5)[:, 0:F], ACT.Silu).then_inc(sil_ready, 1)
                act.wait_ge(ht_ps, g + 1)
                if g >= 2:
                    act.wait_ge(down_ps, g - 1)
                act.activation(ht[:, g % 2, :], bank(6)[0:F, 0:P], ACT.Copy).then_inc(ht_ready, 1)
                act.wait_ge(down_ps, g + 1)
                act.wait_ge(gate_ready, g + 1)
                if g >= 2:
                    act.wait_ge(comb_ps, g - 1)
                act.activation(y3[:, g % 2, 0, :], bank(7)[:, 0:C], ACT.Copy,
                               scale=gate[:, g:g + 1]).then_inc(yh_ready, 1)

        @block.tensor
        def _(pe):
            def transpose_x(b):
                pe.wait_ge(xn_ready, HT * (b + 1))
                if b == 0:
                    pe.wait_ge(id_ready, 1)
                if b >= 2:
                    pe.wait_ge(xt_ready, b - 1)
                for t in range(HT):
                    for k in range(KC):
                        mm = pe.transpose(bank(b % 2)[:, k * T + t * P:k * T + (t + 1) * P],
                                          xn[:, b % 2, t, k * P:(k + 1) * P], id32[:, :])
                mm.then_inc(xt_ps, 1)

            def qkv(b):
                pe.wait_ge(xt_ready, b + 1)
                if b == 0:
                    pe.wait_ge(scaled, 2)
                if b >= 2:
                    pe.wait_ge(r_ready, 4 * (b - 1))
                for m in range(4):
                    for k in range(KC):
                        mm = pe.matmul(ps[1 + b % 2][:, m * T:(m + 1) * T], w_qk[:, k, m * P:(m + 1) * P],
                                       xnt[:, b % 2, k, :], start=(k == 0), stop=(k == KC - 1))
                mm.then_inc(qk_ps, 1)
                if b == 0:
                    pe.wait_ge(wv_in, 16)
                if b >= 2:
                    pe.wait_ge(v_ready, 4 * (b - 1))
                for t in range(HT):
                    for k in range(KC):
                        mm = pe.matmul(bank(6 + b % 2)[:, t * C:(t + 1) * C], xnt[:, b % 2, k, t * P:(t + 1) * P],
                                       w_v[:, k, :], start=(k == 0), stop=(k == KC - 1))
                mm.then_inc(v_ps, 1)

            transpose_x(0)
            for b in range(B):
                if b + 1 < B:
                    transpose_x(b + 1)
                qkv(b)

            def scores(u, p):
                b, g, n = u // 2, u % 2, PIECES * u + p
                if n == 0:
                    pe.wait_ge(attn_const, ATTN_CONSTS)
                    pe.wait_ge(xt_ready, B)
                if p == 0 and g == 0:
                    pe.wait_ge(packed[b], 16 * N_PACK)
                if n >= 2:
                    pe.wait_ge(max_done, n - 1)
                nh, w, qt = (4, P, 0) if p < 2 else (2, T, 1)
                h0 = 4 * p if p < 2 else 2 * (p - 2)
                o = bank(p % 2).rearrange("q (h k) -> q h k", k=w)
                pe.matmul(o[:, :, w - P:w], id16[:, :], causal[:, :].unsqueeze(1).to_broadcast([P, nh, P]),
                          start=True, stop=False, skip_group_check=True)
                for h in range(nh):
                    mm = pe.matmul(o[:, h, :], q_of(b, g, h0 + h, qt * P, (qt + 1) * P, KP),
                                   k_of(b, g, h0 + h, 0, w, KP), start=False, stop=(h == nh - 1),
                                   skip_group_check=True)
                mm.then_inc(s_ps, 1)

            def negmax(u):
                pe.wait_ge(nmp_ready, u + 1)
                misc_wait("negmax", u)
                o = misc[0:2 * HG, 0:P].bitcast(BF16)
                for t in range(HT):
                    mm = pe.transpose(o[:, t * P:(t + 1) * P],
                                      nmp[:, u % 2, t, :, :].rearrange("p a h -> p (a h)"), id16[:, :])
                mm.then_inc(misc_ps, 1)

            def misc_wait(kind, n):
                if MISC[kind, n]:
                    pe.wait_ge(misc_free, MISC[kind, n])
                else:
                    pe.wait_ge(v_ready, 4 * B)

            def scores_t(u, j):
                b, g, n = u // 2, u % 2, STP * u + j
                if j == 0:
                    pe.wait_ge(negrow_in[u % 2], 16 * (u // 2 + 1))
                if n == 0:
                    pe.wait_ge(r_ready, 4 * B)
                    pe.wait_ge(h_ready, 4 * B)
                if n >= 2:
                    pe.wait_ge(exp_done, n - 1)
                o = ps[1 + n % 2]
                if j < 2:
                    for h in range(4):
                        mm = pe.matmul(o[:, h * T:(h + 1) * T], k_of(b, g, 4 * j + h, 0, P, KP + 2),
                                       q_of(b, g, 4 * j + h, 0, T, KP + 2), start=True, stop=True)
                else:
                    for h in range(HG):
                        mm = pe.matmul(o[:, h * P:(h + 1) * P], k_of(b, g, h, P, T, KP + 2),
                                       q_of(b, g, h, P, T, KP + 2), start=True, stop=True)
                mm.then_inc(st_ps, 1)

            def pv(u, sums):
                b, g = u // 2, u % 2
                if not sums:
                    pe.wait_ge(causal_done, STP * (u + 1))
                    if u == 0:
                        pe.wait_ge(v_ready, 4 * B)
                    else:
                        pe.wait_ge(yt_ready, u)
                c0 = T if sums else 0
                for par in range(2):
                    for kt in range(HT):
                        for q in range(4):
                            h = 2 * q + par
                            w = oz[:, par, :] if sums else vz[:, kt * B + b, HG * g + h, :]
                            buf = STP * u + (h // 4 if kt == 0 else 2)
                            n = T if kt == 0 else P
                            hh0 = (h % 4 if kt == 0 else h) * n
                            mm = pe.matmul(bank(6)[32 * q:32 * q + 32, c0 + kt * P:c0 + T], w,
                                           pt[:, buf % (2 * STP), hh0:hh0 + n],
                                           start=(par == 0 and kt == 0 and not sums), stop=(par == 1 and kt == 1),
                                           skip_group_check=True)
                if sums:
                    mm.then_inc(pv_ps, 1)

            def project(b):
                pe.wait_ge(yt_ready, 2 * b + 2)
                misc_wait("proj", b)
                for t in range(HT):
                    for k in range(KC):
                        mm = pe.matmul(misc[:, t * C:(t + 1) * C], y_t[:, b % 2, k, t * P:(t + 1) * P],
                                       w_proj[:, k, :], start=(k == 0), stop=(k == KC - 1))
                mm.then_inc(misc_ps, 1)

            def transpose_xn2(b):
                pe.wait_ge(xn2_ready, HT * (b + 1))
                misc_wait("xt", b)
                for t in range(HT):
                    for k in range(KC):
                        mm = pe.transpose(misc[:, k * T + t * P:k * T + (t + 1) * P],
                                          rows[:, t * B + b, k * P:(k + 1) * P], id32[:, :])
                mm.then_inc(misc_ps, 1)

            def logits(b):
                misc_wait("logits", b)
                for t in range(HT):
                    for k in range(KC):
                        mm = pe.matmul(misc[:, t * E:(t + 1) * E], xt2[:, k, t * P:(t + 1) * P], w_rt[:, k, :],
                                       start=(k == 0), stop=(k == KC - 1))
                mm.then_inc(misc_ps, 1)

            for s in range(LAST_STEP + 1):
                live = s < NU
                if live:
                    scores(s, 0)
                    scores(s, 1)
                for b in range(B):
                    if s == 2 * b + 7:
                        logits(b)
                if 2 <= s < NU + 2:
                    scores_t(s - 2, 0)
                if 1 <= s <= NU:
                    negmax(s - 1)
                if live:
                    scores(s, 2)
                if 3 <= s < NU + 3:
                    pv(s - 3, False)
                if live:
                    scores(s, 3)
                for b in range(B):
                    if s == 2 * b + 5:
                        project(b)
                if 2 <= s < NU + 2:
                    scores_t(s - 2, 1)
                if live:
                    scores(s, 4)
                if 3 <= s < NU + 3:
                    pv(s - 3, True)
                if live:
                    scores(s, 5)
                for b in range(B):
                    if s == 2 * b + 6:
                        transpose_xn2(b)
                if 2 <= s < NU + 2:
                    scores_t(s - 2, 2)

            pe.wait_ge(sel_ready, B)
            pe.wait_ge(moe_const, MOE_CONSTS)
            pe.wait_ge(exp_done, STP * NU)
            for half in range(HT):
                srcs = [(t, ones[:, :]) for t in range(B * half)]
                srcs += [(half * B + b, before[:, 3 - b:7 - b, :].rearrange("p a t -> p (a t)")) for b in range(B)]
                for n, (t, r) in enumerate(srcs):
                    mm = pe.matmul(bank(2 + half)[0:E, :], sel[:, t, :], r, start=(n == 0), stop=(n == len(srcs) - 1))
                mm.then_inc(cum_ps, 1)
            pe.wait_ge(cumc_ready, HT)
            pe.wait_ge(misc_free, len(MISC))
            for g in range(NG):
                if g >= 3:
                    if (g - 3) % 2 == 0:
                        pe.wait_ge(count_dve, (g - 3) // 2 + 1)
                    else:
                        pe.wait_ge(count_act, (g - 3) // 2 + 1)
                for half in range(HT):
                    mm = pe.matmul(ps[SPREAD[g % 3]][:, half * 512:(half + 1) * 512], spread[:, g, :],
                                   cumc[:, half * 512:(half + 1) * 512], start=True, stop=True)
                mm.then_inc(spread_ps, 1)

            pe.wait_ge(count_dve, NG // 2)
            pe.wait_ge(count_act, NG // 2)

            def transpose_rows(g):
                pe.wait_ge(row_in[g % 4], 16 * (g // 4 + 1))
                if g:
                    pe.wait_ge(xg_ready, g)
                for k in range(KC):
                    mm = pe.transpose(bank(4)[:, k * P:(k + 1) * P], grow[:, g % 4, k * P:(k + 1) * P], id32[:, :])
                mm.then_inc(xg_ps, 1)

            def combine(g, n):
                if n == 0:
                    pe.wait_ge(hot_ready, g + 1)
                    pe.wait_ge(yh_ready, g + 1)
                elif n == 1:
                    pe.wait_ge(ym_ready, g + 1)
                else:
                    pe.wait_ge(yl_ready, g + 1)
                for t in range(NT):
                    mm = pe.matmul(bank(t // 2)[:, (t % 2) * C:(t % 2 + 1) * C], onehot[:, g % 2, t * P:(t + 1) * P],
                                   y3[:, g % 2, n, :], start=(g == 0 and n == 0 and t % 2 == 0),
                                   stop=(g == NG - 1 and n == 2), skip_group_check=True)
                    if n == 2 and (t == NT - 1 or (g == NG - 1 and t % 2)):
                        mm.then_inc(comb_ps, 1)

            transpose_rows(0)
            for g in range(NG + 1):
                if g < NG:
                    pe.wait_ge(xg_ready, g + 1)
                    pe.wait_ge(w13_in[g], 16)
                    if g:
                        pe.wait_ge(hh_ready, g)
                    for k in range(KC):
                        for q in range(EG):
                            mm = pe.matmul(bank(5)[q * CAP:(q + 1) * CAP, 0:2 * F],
                                           xgt[:, g % 2, k, q * CAP:(q + 1) * CAP], w13_sb[g][:, q, k, :],
                                           start=(k == 0), stop=(k == KC - 1))
                    mm.then_inc(up_ps, 1)
                if g:
                    combine(g - 1, 0)
                if g < NG:
                    pe.wait_ge(hh_ready, g + 1)
                    if g:
                        pe.wait_ge(ht_ready, g)
                    pe.transpose(bank(6)[0:F, 0:P], hh[:, :], id32[:, :]).then_inc(ht_ps, 1)
                if g:
                    combine(g - 1, 1)
                if g + 1 < NG:
                    transpose_rows(g + 1)
                if g < NG:
                    pe.wait_ge(ht_ready, g + 1)
                    pe.wait_ge(w2_in[g], 16)
                    if g:
                        pe.wait_ge(yr_ready, g)
                    for q in range(EG):
                        mm = pe.matmul(bank(7)[q * CAP:(q + 1) * CAP, 0:C], ht[:, g % 2, q * CAP:(q + 1) * CAP],
                                       w2_sb[g % W2S][:, q, :], start=True, stop=True)
                    mm.then_inc(down_ps, 1)
                if g:
                    combine(g - 1, 2)

        @block.vector
        def _(dve):
            steps = [0]

            def link(ins):
                steps[0] += 1
                ins.then_inc(dve_step, 1)
                dve.wait_ge(dve_step, steps[0])

            def moments(b, buf):
                for t in range(HT):
                    link(dve.bn_stats(stats[:, buf, t, :], x_sb[:, t * B + b, :]))
                    link(dve.bn_aggr(mv[:, buf, t, :], stats[:, buf, t, :]))
                return dve.tensor_scalar(ve[:, buf, :], mv[:, buf, :, 1], EPS, None, ALU.add)

            def norm1(b):
                dve.wait_ge(x_in[b], 16)
                moments(b, b % 2).then_inc(var_ready, 1)
                dve.wait_ge(rstd_ready, b + 1)
                if b >= 2:
                    dve.wait_ge(xt_ps, b - 1)
                for t in range(HT):
                    dve.tensor_scalar(xn[:, b % 2, t, :], x_sb[:, t * B + b, :], mv[:, b % 2, t, 0:1],
                                      rstd[:, b % 2, t:t + 1], ALU.subtract, ALU.mult).then_inc(xn_ready, 1)

            norm1(0)
            dve.wait_ge(wqk_in, 16)
            dve.wait_ge(bqk_in, 16)
            dve.tensor_scalar(w_qk[:, :, 0:C], w_qk[:, :, 0:C], SCALE, None, ALU.mult).then_inc(scaled, 1)
            dve.tensor_scalar(b_qk[:, 0:2], b_qk[:, 0:2], SCALE, None, ALU.mult).then_inc(scaled, 1)
            norm1(1)
            for b in range(B):
                if b >= 2:
                    dve.wait_ge(l_ready, b - 1)
                for m in range(4):
                    dve.wait_ge(h_ready, 4 * b + 2 * (m // 2) + 2)
                    dve.scalar_tensor_tensor(out=res[:, b % 2, m, :], in0=ps[1 + b % 2][:, m * T:(m + 1) * T],
                                             scalar=b_qk[:, m:m + 1],
                                             in1=spl[:, b % 2, m // 2, (m % 2) * T:(m % 2 + 1) * T],
                                             op0=ALU.add, op1=ALU.subtract).then_inc(r_ready, 1)
                dve.wait_ge(v_ps, b + 1)
                if b == 0:
                    dve.wait_ge(zeroed, 1)
                    dve.wait_ge(small_in, N_SMALL)
                for t in range(HT):
                    for par in range(2):
                        pv_in = bank(6 + b % 2)[:, t * C:(t + 1) * C].rearrange("p (h a d) -> p h a d", a=2, d=D)
                        bias = b_v[:, :].rearrange("p (h a d) -> p h a d", a=2, d=D)
                        dve.tensor_tensor(vz[:, t * B + b, par::2, par * D:(par + 1) * D], pv_in[:, :, par, :],
                                          bias[:, :, par, :], ALU.add).then_inc(v_ready, 1)
                if b + 2 < B:
                    norm1(b + 2)

            def row_max(u, p):
                n = PIECES * u + p
                dve.wait_ge(s_ps, n + 1)
                w, qt = (P, 0) if p < 2 else (T, 1)
                h0, nh = (4 * p, 4) if p < 2 else (2 * (p - 2), 2)
                dve.tensor_reduce(nm[:, u % 2, qt, h0:h0 + nh], bank(p % 2).rearrange("q (h k) -> q h k", k=w),
                                  AX.X, ALU.max, negate=True).then_inc(max_done, 1)

            def negmax_parts(u):
                dve.wait_ge(max_done, PIECES * (u + 1))
                if u >= 2:
                    dve.wait_ge(misc_ps, MISC["negmax", u - 2] + 1)
                link(dve.tensor_copy(nmp[:, u % 2, :, 0, :], nm[:, u % 2, :, :]))
                dve.tensor_tensor(nmp[:, u % 2, :, 1, :], nm[:, u % 2, :, :], nmp[:, u % 2, :, 0, :],
                                  ALU.subtract).then_inc(nmp_ready, 1)

            def normalise(u):
                b, g = u // 2, u % 2
                dve.wait_ge(pv_ps, u + 1)
                if b >= 2 and g == 0:
                    dve.wait_ge(misc_ps, MISC["proj", b - 2] + 1)
                link(dve.reciprocal(rden[:, :], bank(6)[:, T:2 * T]))
                dve.tensor_tensor(y_t[:, b % 2, g, :], bank(6)[:, 0:T], rden[:, :], ALU.mult).then_inc(yt_ready, 1)

            def residual_norm2(b):
                dve.wait_ge(misc_ps, MISC["proj", b] + 1)
                dve.wait_ge(xb_ready, HT * (b + 1))
                dve.tensor_tensor(x_sb[:, b::B, :], misc.rearrange("p (t c) -> p t c", t=HT), x_sb[:, b::B, :],
                                  ALU.add).then_inc(misc_free, 1)
                dve.wait_ge(misc_free, MISC["proj", b] + 1)
                moments(b, b % 2).then_inc(var2_ready, 1)
                dve.wait_ge(rstd2_ready, b + 1)
                for t in range(HT):
                    dve.tensor_scalar(rows[:, t * B + b, 0:C], x_sb[:, t * B + b, :], mv[:, b % 2, t, 0:1],
                                      rstd[:, b % 2, t:t + 1], ALU.subtract, ALU.mult).then_inc(xn2_ready, 1)

            def choose(b):
                dve.wait_ge(misc_free, MISC["logits", b] + 1)
                for t in range(HT):
                    link(dve.max(m8[:, t, :], lg[:, t, :]))
                    link(dve.match_replace(lr[:, t, :], m8[:, t, :], lg[:, t, :], -3.0e38))
                if b:
                    dve.wait_ge(e_ready, HT * b)
                dve.tensor_scalar(negm[:, :], m8[:, 0:HT, 0], -1.0, None, ALU.mult).then_inc(negm_ready, 1)
                dve.tensor_tensor(sel[:, b::B, :], lr[:, :, :], lg[:, :, :], ALU.not_equal).then_inc(sel_ready, 1)

            def expert_weights(b):
                dve.wait_ge(e_ready, HT * (b + 1))
                dve.wait_ge(sel_ready, b + 1)
                link(dve.tensor_tensor(lr[:, :, :], ee[:, :, :], sel[:, b::B, :], ALU.mult))
                link(dve.tensor_reduce(wsum[:, :], lr[:, :, :], AX.X, ALU.add))
                link(dve.reciprocal(wrec[:, :], wsum[:, :]))
                for t in range(HT):
                    ins = dve.tensor_scalar(rows[:, t * B + b, C:ROW], lr[:, t, :], wrec[:, t:t + 1], None, ALU.mult)
                    if t == HT - 1:
                        ins.then_inc(rows_ready, 1)
                    else:
                        link(ins)

            for s in range(LAST_STEP + 1):
                if s < NU:
                    for p in range(PIECES):
                        row_max(s, p)
                    negmax_parts(s)
                if 3 <= s < NU + 3:
                    normalise(s - 3)
                for b in range(B):
                    if s == 2 * b + 8:
                        expert_weights(b)
                for b in range(B):
                    if s == 2 * b + 5:
                        residual_norm2(b)
                    if s == 2 * b + 7:
                        choose(b)

            dve.wait_ge(moe_const, MOE_CONSTS)
            link(dve.tensor_reduce(slot_c[:, 0:1], pc[:, :], AX.X, ALU.add))
            dve.tensor_scalar(slot_c[:, 1:2], slot_c[:, 0:1], 0.5, None, ALU.add).then_inc(slotc_ready, 1)
            dve.wait_ge(pv_ps, NU)
            for half in range(HT):
                dve.wait_ge(cum_ps, half + 1)
                dve.tensor_scalar(cumc[:, half * 512:(half + 1) * 512], bank(2 + half)[0:E, :], 2.0 * CAP, None,
                                  ALU.min).then_inc(cumc_ready, 1)
            for g in range(0, NG, 2):
                dve.wait_ge(spread_ps, g + 1)
                if g:
                    dve.wait_ge(count_dve, g // 2)
                dve.tensor_scalar(junk[:, 0, :], ps[SPREAD[g % 3]][:, :], slot_c[:, 0:1], 0.0, ALU.is_le, ALU.add,
                                  accum_out=tok_n[:, g:g + 1]).then_inc(count_dve, 1)
                if g % 4 == 2:
                    dve.wait_ge(count_act, g // 2 + 1)
                    dve.wait_ge(count_dve, g // 2 + 1)
                    odd = tok_n[:, g - 1:g + 2:2]
                    link(dve.tensor_scalar(odd, odd, 0.5, NTOK / 2, ALU.mult, ALU.add))
                    dve.tensor_scalar(tok_i[:, g - 2:g + 2], tok_n[:, g - 2:g + 2], NTOK - 1.0, None, ALU.min)\
                        .then_inc(tok_ready, 1)

            def take_rows(g):
                dve.wait_ge(row_in[g % 4], 16 * (g // 4 + 1))
                link(dve.tensor_tensor(g4[:, :], grow[:, g % 4, C + EG * g:C + EG * (g + 1)], eq4[:, :], ALU.mult))
                dve.tensor_reduce(gate[:, g:g + 1], g4[:, :], AX.X, ALU.add).then_inc(gate_ready, 1)
                dve.wait_ge(xg_ps, g + 1)
                if g >= 2:
                    dve.wait_ge(up_ps, g - 1)
                dve.tensor_copy(xgt[:, g % 2, :, :].rearrange("p k t -> p (k t)"), bank(4)[:, 0:KC * P])\
                    .then_inc(xg_ready, 1)

            take_rows(0)
            for g in range(NG):
                dve.wait_ge(sil_ready, g + 1)
                if g:
                    dve.wait_ge(ht_ps, g)
                dve.tensor_tensor(hh[:, :], bank(5)[:, F:2 * F], sil[:, :], ALU.mult).then_inc(hh_ready, 1)
                if g >= 2:
                    dve.wait_ge(comb_ps, g - 1)
                dve.tensor_scalar(onehot[:, g % 2, :], tokid[:, :], tok_n[:, g:g + 1], None, ALU.is_equal)\
                    .then_inc(hot_ready, 1)
                if g + 1 < NG:
                    take_rows(g + 1)
                dve.wait_ge(yh_ready, g + 1)
                dve.scalar_tensor_tensor(out=yr[:, :], in0=bank(7)[:, 0:C], scalar=gate[:, g:g + 1],
                                         in1=y3[:, g % 2, 0, :], op0=ALU.mult, op1=ALU.subtract)\
                    .then_inc(yr_ready, 1)
                dve.wait_ge(yr_ready, g + 1)
                dve.tensor_copy(y3[:, g % 2, 1, :], yr[:, :]).then_inc(ym_ready, 1)
                dve.wait_ge(ym_ready, g + 1)
                dve.tensor_tensor(y3[:, g % 2, 2, :], yr[:, :], y3[:, g % 2, 1, :], ALU.subtract)\
                    .then_inc(yl_ready, 1)
                dve.wait_ge(yl_ready, g + 1)
            for n in range(4):
                dve.wait_ge(comb_ps, NG + n)
                dve.tensor_tensor(x_sb[:, 2 * n:2 * n + 2, :], bank(n).rearrange("p (t c) -> p t c", t=2),
                                  x_sb[:, 2 * n:2 * n + 2, :], ALU.add).then_inc(fin_ready, 1)


_INS = ["x", "wqk", "bqk", "wv", "bv", "wproj", "bproj", "rwt", "w13", "w2"]


def kernel(L0_attn_x, L0_attn_w_attn, L0_attn_b_attn, L0_attn_w_proj, L0_attn_b_proj, L0_ffn_router_w, L0_ffn_w1,
           L0_ffn_v1, L0_ffn_w2):
    import numpy as np
    import concourse.bacc as bacc
    from concourse.bass_utils import run_bass_kernel_spmd

    def a(v):
        return np.ascontiguousarray(v)

    qk = np.asarray(L0_attn_w_attn)[:, :2 * C].reshape(C, 2, 2, HG, D).transpose(0, 1, 2, 4, 3).reshape(C, 2 * C)
    bqk = np.asarray(L0_attn_b_attn)[:2 * C].reshape(4, HG, D).transpose(2, 1, 0).reshape(P, 4)
    w1 = np.asarray(L0_ffn_w1).reshape(NG, EG, F, KC, P)
    v1 = np.asarray(L0_ffn_v1).reshape(NG, EG, F, KC, P)
    w13 = np.concatenate([w1, v1], axis=2).transpose(0, 4, 1, 3, 2)
    w2 = np.asarray(L0_ffn_w2).reshape(NG, EG, F, C).transpose(0, 2, 1, 3)
    host = {
        "x": a(L0_attn_x), "wqk": a(qk), "bqk": a(bqk), "wv": a(np.asarray(L0_attn_w_attn)[:, 2 * C:]),
        "bv": a(np.asarray(L0_attn_b_attn)[2 * C:]), "wproj": a(L0_attn_w_proj), "bproj": a(L0_attn_b_proj),
        "rwt": a(np.asarray(L0_ffn_router_w).T), "w13": a(w13), "w2": a(w2),
    }
    nc = bacc.Bacc("TRN2", target_bir_lowering=False, num_devices=1)
    args = [nc.dram_tensor(f"in_{n}", host[n].shape, mybir.dt.from_np(host[n].dtype), kind="ExternalInput").ap()
            for n in _INS]
    out = nc.dram_tensor("out_0", (B, T, C), F32, kind="ExternalOutput").ap()
    build(nc, *args, out)
    r = run_bass_kernel_spmd(nc, [{f"in_{n}": host[n] for n in _INS}], core_ids=[0])
    return r.results[0]["out_0"]
```

```python
from contextlib import ExitStack

import concourse.bass as bass
from concourse import mybir

F32 = mybir.dt.float32
BF16 = mybir.dt.bfloat16
F16 = mybir.dt.float16
U32 = mybir.dt.uint32
ALU = mybir.AluOpType
ACT = mybir.ActivationFunctionType
AX = mybir.AxisListType

P = 128
B, T, C = 4, 256, 256
H, D = 16, 16
E, TOPK, F, CAP = 64, 8, 96, 32
KC = C // P
HT = T // P
NT = B * HT
HG = 8
NU = B * H // HG
PARTS = [(0, 0), (0, 1), (1, 0), (1, 1), (0, 2), (2, 0)]
KP = D * len(PARTS)
EPS = 1e-5
SCALE = D ** -0.5
MASKED = -1e30
EG = P // CAP
NG = E // EG
ROW = C + E
NTOK = B * T
W2S = 9
PIECES = 6
STP = 3
WARM_UP = 11
LAST_STEP = 2 * (B - 1) + 6
N_PACK = 1 + len(PARTS) + sum(pq > pk for pq, pk in PARTS)
ATTN_CONSTS = 2
MOE_CONSTS = 5
SPREAD = [2, 3, 0]


def misc_schedule():
    use = {}
    for s in range(LAST_STEP + 1):
        for b in range(B):
            if s == 2 * b + 6:
                use["logits", b] = len(use)
            if s == 2 * b + 5:
                use["proj", b] = len(use)
        if 1 <= s <= NU:
            use["negmax", s - 1] = len(use)
        for b in range(B):
            if s == 2 * b + 5:
                use["xt", b] = len(use)
    return use


def build(nc, x, wqk, bqk, wv, bv, wproj, bproj, rwt, w13, w2, out):
    with ExitStack() as ctx:
        ent = ctx.enter_context

        def sb(name, shape, dt):
            return ent(nc.sbuf_tensor(name, shape, dt))

        def sem(name):
            return ent(nc.semaphore(name))

        x_sb = sb("x_sb", [P, NT, C], F32)
        rows = sb("rows", [P, NT, ROW], F32)
        id32 = sb("id32", [P, P], F32)
        id16 = sb("id16", [P, P], BF16)
        causal = sb("causal", [P, P], BF16)
        before = sb("before", [P, 7, P], BF16)
        ones = sb("ones", [P, 4 * P], BF16)
        spread = sb("spread", [E, NG, P], BF16)
        tokid = sb("tokid", [P, NTOK], F16)
        w_proj = sb("w_proj", [P, KC, C], F32)
        w_rt = sb("w_rt", [P, KC, E], F32)
        b_v = sb("b_v", [P, C], F32)
        b_proj = sb("b_proj", [P, C], F32)
        b_qk = sb("b_qk", [P, 4], F32)
        stats = sb("stats", [P, B, HT, 6], F32)
        mv = sb("mv", [P, B, HT, 2], F32)
        ve = sb("ve", [P, B, HT], F32)
        rstd = sb("rstd", [P, B, HT], F32)
        mhalf = sb("mhalf", [P, HT], F32)
        sel = sb("sel", [P, NT, E], BF16)
        slot_c = sb("slot_c", [P, 2], F32)
        pc = sb("pc", [P, EG], F32)
        eq4 = sb("eq4", [P, EG], F32)
        tok_n = sb("tok_n", [P, NG], F32)
        tok_i = sb("tok_i", [P, NG], U32)
        m8 = sb("m8", [P, NT, 8], F32)
        negm = sb("negm", [P, HT], F32)
        wsum = sb("wsum", [P, HT], F32)
        wrec = sb("wrec", [P, HT], F32)
        lg = sb("lg", [P, HT, E], F32)
        lr = sb("lr", [P, HT, E], F32)
        ee = sb("ee", [P, HT, E], F32)
        nm = sb("nm", [P, 2, HT, HG], F32)
        nmp = sb("nmp", [P, 2, HT, 2, HG], BF16)
        nmt = sb("nmt", [2 * HG, 2, T], BF16)
        y_t = sb("y_t", [P, 2, KC, T], F32)
        yv = sb("yv", [P, 2, T], F32)
        rden = sb("rden", [P, HT * HG], F32)
        yn = sb("yn", [P, HT * HG, D], F32)
        xt2 = sb("xt2", [P, KC, T], F32)

        size = {F32: 4, BF16: 2, F16: 2}
        at = [(nc.sbuf_base + 31) // 32 * 32]
        words = (nc.sbuf_bytes_remaining - 256) // 4
        top = at[0] + 4 * words - 64
        sb("arena", [P, words], F32)

        def place(name, shape, dt, offset=None):
            n = size[dt]
            for d in shape[1:]:
                n *= d
            n = (n + 31) // 32 * 32
            if offset is None:
                offset = at[0]
                at[0] += n
                assert at[0] <= top, (name, at[0], top)
            return nc.alloc_sbuf_tensor_at(name, shape, dt, offset=offset)

        W13B, W2B = EG * KC * 2 * F * 4, EG * C * 4
        w13_at, w2_at = {}, {}
        pack, pack_at = [], []
        for b in range(B):
            pack_at.append(at[0])
            pack.append(place(f"pack{b}", [KP + 2, HG, 2, 2, T], BF16))
            w13_at[8 + 2 * b] = pack_at[b]
            w13_at[9 + 2 * b] = pack_at[b] + W13B
            w2_at[1 + b] = pack_at[b] + 2 * W13B
        vz_at = at[0]
        vz = place("vz", [P, NT, H, 32], F32)
        for n in range(4):
            w2_at[5 + n] = vz_at + n * W2B
        pt_at = at[0]
        pt = place("pt", [P, 2 * STP, 1024], F32)
        xn = nc.alloc_sbuf_tensor_at("xn", [P, B, HT, C], F32, offset=pt_at)
        a_at = at[0]
        w_qk = place("w_qk", [P, KC, 2 * C], F32)
        w_v = place("w_v", [P, KC, C], F32)
        xnt = place("xnt", [P, 2, KC, T], F32)
        spl = place("spl", [P, 2, 3 * 2, 2 * T], BF16)
        res = place("res", [P, 2, 4, T], F32)
        a_end = at[0] = max(at[0], a_at + 5 * W13B + W2B)
        free_chunks = min(3, (top - a_end) // W13B)
        for n in range(5):
            w13_at[free_chunks + n] = a_at + n * W13B
        w2_at[0] = a_at + 5 * W13B
        for n in range(free_chunks):
            w13_at[n] = a_end + n * W13B
        assert free_chunks == 3
        w13_sb = [nc.alloc_sbuf_tensor_at(f"w13_{g}", [P, EG, KC, 2 * F], F32, offset=w13_at[g]) for g in range(NG)]
        w2_sb = [nc.alloc_sbuf_tensor_at(f"w2_{g}", [F, EG, C], F32, offset=w2_at[g]) for g in range(W2S)]
        d_at = at[0]
        at[0] = pt_at
        cumc = place("cumc", [E, NTOK], BF16)
        junk = place("junk", [P, 2, NTOK], BF16)
        grow = place("grow", [P, 4, ROW], F32)
        xgt = place("xgt", [P, 2, KC, P], F32)
        sil = place("sil", [P, F], F32)
        hh = place("hh", [P, F], F32)
        ht = place("ht", [F, 2, P], F32)
        y3 = place("y3", [P, 2, 3, C], BF16)
        yr = place("yr", [P, C], F32)
        g4 = place("g4", [P, EG], F32)
        gate = place("gate", [P, NG], F32)
        assert at[0] <= a_at
        onehot = junk
        at[0] = d_at

        xrow = nc.dram_tensor("xrow", [NTOK, ROW], F32, kind="Internal").ap()

        ps = [ent(nc.psum_tensor(f"pair{n}", [P, 1024], F32)) for n in range(4)]

        def bank(n):
            return ps[n // 2][:, (n % 2) * 512:(n % 2) * 512 + 512]

        x_in = [sem(f"x_in{b}") for b in range(B)]
        wqk_in, wv_in, bqk_in, small_in = sem("wqk_in"), sem("wv_in"), sem("bqk_in"), sem("small_in")
        scaled = sem("scaled")
        ones_ready, slotc_ready = sem("ones_ready"), sem("slotc_ready")
        v_ones, id_ready, attn_const, moe_const = sem("v_ones"), sem("id_ready"), sem("attn_const"), sem("moe_const")
        var_ready, rstd_ready, xn_ready = sem("var_ready"), sem("rstd_ready"), sem("xn_ready")
        xt_ps, xt_ready = sem("xt_ps"), sem("xt_ready")
        qk_ps, v_ps = sem("qk_ps"), sem("v_ps")
        h_ready, r_ready, m_ready, l_ready, v_ready = (sem("h_ready"), sem("r_ready"), sem("m_ready"),
                                                       sem("l_ready"), sem("v_ready"))
        packed = [sem(f"packed{b}") for b in range(B)]
        xb_ready = sem("xb_ready")
        s_ps, max_done = sem("s_ps"), sem("max_done")
        nmp_ready = sem("nmp_ready")
        negrow_in = [sem(f"negrow_in{n}") for n in range(2)]
        st_ps, exp_done, causal_done = sem("st_ps"), sem("exp_done"), sem("causal_done")
        pv_ps, yv_ready, yv_ps, yn_ready, yt_ps, yt_ready = (sem("pv_ps"), sem("yv_ready"), sem("yv_ps"),
                                                             sem("yn_ready"), sem("yt_ps"), sem("yt_ready"))
        misc_ps, misc_free = sem("misc_ps"), sem("misc_free")
        var2_ready, rstd2_ready, xn2_ready = sem("var2_ready"), sem("rstd2_ready"), sem("xn2_ready")
        negm_ready, e_ready, sel_ready, rows_ready = (sem("negm_ready"), sem("e_ready"), sem("sel_ready"),
                                                      sem("rows_ready"))
        rows_out = [sem(f"rows_out{b}") for b in range(B)]
        cum_ps, cumc_ready = sem("cum_ps"), sem("cumc_ready")
        spread_ps, count_dve, count_act, tok_ready = (sem("spread_ps"), sem("count_dve"), sem("count_act"),
                                                      sem("tok_ready"))
        row_in = [sem(f"row_in{n}") for n in range(4)]
        w13_in = [sem(f"w13_in{g}") for g in range(NG)]
        w2_in = [sem(f"w2_in{g}") for g in range(NG)]
        xg_ps, xg_ready, gate_ready = sem("xg_ps"), sem("xg_ready"), sem("gate_ready")
        up_ps, sil_ready, hh_ready = sem("up_ps"), sem("sil_ready"), sem("hh_ready")
        ht_ps, ht_ready, down_ps = sem("ht_ps"), sem("ht_ready"), sem("down_ps")
        yh_ready, yr_ready, ym_ready, yl_ready = sem("yh_ready"), sem("yr_ready"), sem("ym_ready"), sem("yl_ready")
        hot_ready, comb_ps, fin_ready, out_done = sem("hot_ready"), sem("comb_ps"), sem("fin_ready"), sem("out_done")
        dve_step = sem("dve_step")
        pool_step = sem("pool_step")

        MISC = misc_schedule()
        misc = bank(7)
        N_SMALL = 4 * 16
        q_of = lambda b, g, h, lo, hi, k: pack[b][0:k, h, 0, g, lo:hi]
        k_of = lambda b, g, h, lo, hi, k: pack[b][0:k, h, 1, g, lo:hi]

        block = ent(nc.Block())

        @block.sync
        def _(sp):
            def load_w13(g):
                sp.dma_start(w13_sb[g][:, :, :, :], w13[g]).then_inc(w13_in[g], 16)

            def load_w2(g):
                sp.dma_start(w2_sb[g % W2S][:, :, :], w2[g]).then_inc(w2_in[g], 16)

            def load_x(b):
                sp.dma_start(x_sb[:, b::B, :], x[b].rearrange("(h p) c -> p h c", p=P)).then_inc(x_in[b], 16)

            load_x(0)
            sp.dma_start(w_qk[:, :, :], wqk.rearrange("(k p) n -> p k n", p=P)).then_inc(wqk_in, 16)
            sp.dma_start(b_qk[:, :], bqk).then_inc(bqk_in, 16)
            load_x(1)
            sp.dma_start(w_v[:, :, :], wv.rearrange("(k p) n -> p k n", p=P)).then_inc(wv_in, 16)
            sp.dma_start(b_v[:, :], bv.partition_broadcast(P)).then_inc(small_in, 16)
            sp.dma_start(b_proj[:, :], bproj.partition_broadcast(P)).then_inc(small_in, 16)
            load_x(2)
            load_x(3)
            sp.dma_start(w_proj[:, :, :], wproj.rearrange("(k p) n -> p k n", p=P)).then_inc(small_in, 16)
            sp.dma_start(w_rt[:, :, :], rwt.rearrange("(k p) n -> p k n", p=P)).then_inc(small_in, 16)
            sp.wait_ge(ones_ready, 1)
            for b in range(B):
                sp.dma_start(pack[b][KP:KP + 2, :, 1, :, :].rearrange("r h g t -> r h (g t)"),
                             ones[0:2 * HG, :]).then_inc(packed[b], 16)
            for b in range(B):
                pair = spl[:, b % 2, :, :]
                for n, (pq, pk) in enumerate(PARTS):
                    if n == 0:
                        sp.wait_ge(h_ready, 4 * (b + 1))
                    if n == 1:
                        sp.wait_ge(m_ready, b + 1)
                    if n == 4:
                        sp.wait_ge(l_ready, b + 1)
                    dst = pack[b][n * D:(n + 1) * D, :, :, :, :]
                    iq, ik = 2 * pq, 2 * pk + 1
                    if ik > iq:
                        sp.dma_start(dst.rearrange("d h a g t -> d h (a g t)"),
                                     pair[:, iq:ik + 1:ik - iq, :]).then_inc(packed[b], 16)
                    else:
                        sp.dma_start(dst[:, :, 0, :, :].rearrange("d h g t -> d h (g t)"),
                                     pair[:, iq, :]).then_inc(packed[b], 16)
                        sp.dma_start(dst[:, :, 1, :, :].rearrange("d h g t -> d h (g t)"),
                                     pair[:, ik, :]).then_inc(packed[b], 16)
                if b < 3:
                    load_w13(b)
            late = list(range(3, 8))
            for s in range(1, LAST_STEP + 2):
                if s <= NU:
                    u = s - 1
                    sp.wait_ge(misc_free, MISC["negmax", u] + 1)
                    sp.dma_start(pack[u // 2][KP:KP + 2, :, 0, u % 2, :], nmt[:, u % 2, :])\
                      .then_inc(negrow_in[u % 2], 16)
                if s == 1:
                    for b in range(B):
                        sp.wait_ge(packed[b], 16 * N_PACK)
                    sp.wait_ge(l_ready, B)
                    sp.wait_ge(v_ready, HT * B)
                if late:
                    load_w13(late.pop(0))
                    if not late:
                        load_w2(0)
                for b in range(B):
                    if s == 2 * b + 4:
                        sp.wait_ge(st_ps, STP * (2 * b + 2))
                        load_w13(8 + 2 * b)
                        load_w13(9 + 2 * b)
                        load_w2(1 + b)
                    if s == 2 * b + 7:
                        sp.wait_ge(rows_ready, b + 1)
                        sp.dma_start(xrow.rearrange("(h s b) c -> b s h c", b=B, h=HT)[b],
                                     rows[:, b::B, :]).then_inc(rows_out[b], 16)
                if s == LAST_STEP:
                    sp.wait_ge(pv_ps, NU)
                    for n in range(5, W2S):
                        load_w2(n)
            for g in range(W2S, NG):
                sp.wait_ge(down_ps, g - W2S + 1)
                load_w2(g)
            for n in range(B):
                sp.wait_ge(fin_ready, n + 1)
                for t in range(2 * n, 2 * n + 2):
                    b, half = t % B, t // B
                    sp.dma_start(out[b, half * P:(half + 1) * P, :], x_sb[:, t, :]).then_inc(out_done, 16)
            sp.wait_ge(out_done, 16 * NT)

        @block.gpsimd
        def _(pool):
            steps = [0]

            def link(ins):
                steps[0] += 1
                ins.then_inc(pool_step, 1)
                pool.wait_ge(pool_step, steps[0])

            link(pool.memset(id32[:, :], 0.0))
            pool.affine_select(out=id32[:, :], in_=id32[:, :], compare_op=ALU.not_equal, fill=1.0, base=0,
                               pattern=[[-1, P]], channel_multiplier=1).then_inc(id_ready, 1)
            link(pool.memset(mhalf[:, :], -0.5))

            def pow_rstd(b, ready, done):
                pool.wait_ge(ready, b + 1)
                pool.tensor_tensor(out=rstd[:, b, :], in0=ve[:, b, :], in1=mhalf[:, :],
                                   op=ALU.pow).then_inc(done, 1)

            for b in range(B - 1):
                pow_rstd(b, var_ready, rstd_ready)
                if b == 0:
                    pool.memset(vz[:, 0::B, :, D:], 1.0).then_inc(v_ones, 1)
            for b in range(B):
                pool.wait_ge(m_ready, b + 1)
                if b >= 2:
                    pool.wait_ge(packed[b - 2], 16 * N_PACK)
                pool.tensor_tensor(out=spl[:, b % 2, 4:6, :].rearrange("p a n -> p (a n)"),
                                   in0=res[:, b % 2, :, :].rearrange("p m t -> p (m t)"),
                                   in1=spl[:, b % 2, 2:4, :].rearrange("p a n -> p (a n)"),
                                   op=ALU.subtract).then_inc(l_ready, 1)
                if b == 0:
                    pow_rstd(B - 1, var_ready, rstd_ready)
                    for n in range(1, B):
                        pool.memset(vz[:, n::B, :, D:], 1.0).then_inc(v_ones, 1)
                pool.wait_ge(xn_ready, HT * (b + 1))
                if b == 0:
                    pool.wait_ge(small_in, N_SMALL)
                for t in range(HT):
                    pool.tensor_tensor(out=x_sb[:, t * B + b, :], in0=x_sb[:, t * B + b, :], in1=b_proj[:, :],
                                       op=ALU.add).then_inc(xb_ready, 1)
                if b == 1:
                    link(pool.memset(id16[:, :], 0.0))
                    pool.affine_select(out=id16[:, :], in_=id16[:, :], compare_op=ALU.not_equal, fill=1.0, base=0,
                                       pattern=[[-1, P]], channel_multiplier=1).then_inc(attn_const, 1)
                    link(pool.memset(causal[:, :], 0.0))
                    pool.affine_select(out=causal[:, :], in_=causal[:, :], compare_op=ALU.is_ge, fill=MASKED, base=0,
                                       pattern=[[-1, P]], channel_multiplier=1).then_inc(attn_const, 1)
            link(pool.memset(before[:, :, :], 1.0))
            pool.affine_select(out=before[:, 0:3, :], in_=before[:, 0:3, :], compare_op=ALU.is_gt, fill=0.0, base=0,
                               pattern=[[0, 3], [1, P]], channel_multiplier=-1).then_inc(moe_const, 1)
            pool.affine_select(out=before[:, 3:7, :], in_=before[:, 3:7, :], compare_op=ALU.is_ge, fill=0.0, base=0,
                               pattern=[[0, 4], [1, P]], channel_multiplier=-1).then_inc(moe_const, 1)

            def causal_zero(n):
                pool.wait_ge(exp_done, n + 1)
                buf, j = n % (2 * STP), n % STP
                v = pt[:, buf, :].rearrange("p (h t) -> p h t", t=T if j < 2 else P)[:, :, 0:P]
                pool.affine_select(out=v, in_=v, compare_op=ALU.is_ge, fill=0.0, base=0,
                                   pattern=[[0, 4 if j < 2 else 8], [1, P]], channel_multiplier=-1)\
                    .then_inc(causal_done, 1)

            def moe_consts(part):
                if part == 0:
                    link(pool.memset(spread[:, :, :], 0.0))
                    pool.affine_select(out=spread[:, :, :].rearrange("e g (q c) -> e g q c", q=EG),
                                       in_=spread[:, :, :].rearrange("e g (q c) -> e g q c", q=EG),
                                       compare_op=ALU.not_equal, fill=1.0, base=0,
                                       pattern=[[-EG, NG], [-1, EG], [0, CAP]], channel_multiplier=1)\
                        .then_inc(moe_const, 1)
                elif part == 1:
                    pool.iota(tokid[:, :].rearrange("p (h b s) -> p h b s", h=HT, b=B),
                              pattern=[[P * B, HT], [1, B], [B, P]], base=0, channel_multiplier=0,
                              allow_small_or_imprecise_dtypes=True).then_inc(moe_const, 1)
                elif part == 2:
                    link(pool.memset(eq4[:, :], 1.0))
                    link(pool.affine_select(out=eq4[:, :], in_=eq4[:, :], compare_op=ALU.is_ge, fill=0.0, base=0,
                                            pattern=[[-CAP, EG]], channel_multiplier=1))
                    link(pool.affine_select(out=eq4[:, :], in_=eq4[:, :], compare_op=ALU.is_ge, fill=0.0,
                                            base=CAP - 1, pattern=[[CAP, EG]], channel_multiplier=-1))
                    link(pool.iota(pc[:, :], pattern=[[-CAP, EG]], base=0, channel_multiplier=1,
                                   allow_small_or_imprecise_dtypes=True))
                    pool.tensor_tensor(out=pc[:, :], in0=pc[:, :], in1=eq4[:, :], op=ALU.mult)\
                        .then_inc(moe_const, 1)

            for s in range(LAST_STEP + 1):
                if 2 <= s < NU + 2:
                    causal_zero(STP * (s - 2))
                for b in range(B):
                    if s == 2 * b + 5:
                        pow_rstd(b, var2_ready, rstd2_ready)
                if 2 <= s < NU + 2:
                    causal_zero(STP * (s - 2) + 1)
                    causal_zero(STP * (s - 2) + 2)
                if s < 3:
                    moe_consts(s)

            def gather(g):
                if g % 4 == 0:
                    pool.wait_ge(tok_ready, g // 4 + 1)
                if g == 0:
                    for b in range(B):
                        pool.wait_ge(rows_out[b], 16)
                if g >= 4:
                    pool.wait_ge(xg_ps, g - 3)
                    pool.wait_ge(gate_ready, g - 3)
                pool.indirect_dma_start(out=grow[:, g % 4, :], out_offset=None, in_=xrow,
                                        in_offset=bass.IndirectOffsetOnAxis(ap=tok_i[:, g:g + 1], axis=0))\
                    .then_inc(row_in[g % 4], 16)

            for g in range(NG):
                gather(g)

        @block.scalar
        def _(act):
            def copy_xt(b):
                act.wait_ge(xt_ps, b + 1)
                if b >= 2:
                    act.wait_ge(v_ps, b - 1)
                act.activation(xnt[:, b % 2, :, :].rearrange("p k t -> p (k t)"), bank(b % 2),
                               ACT.Copy).then_inc(xt_ready, 1)

            copy_xt(0)
            act.wait_ge(scaled, 2)
            for b in range(B):
                act.wait_ge(qk_ps, b + 1)
                if b >= 2:
                    act.wait_ge(packed[b - 2], 16 * N_PACK)
                for m in range(4):
                    act.activation(spl[:, b % 2, m // 2, (m % 2) * T:(m % 2 + 1) * T],
                                   ps[1 + b % 2][:, m * T:(m + 1) * T], ACT.Identity,
                                   bias=b_qk[:, m:m + 1]).then_inc(h_ready, 1)
                if b + 1 < B:
                    copy_xt(b + 1)
                act.wait_ge(r_ready, 4 * (b + 1))
                act.activation(spl[:, b % 2, 2:4, :].rearrange("p a n -> p (a n)"),
                               res[:, b % 2, :, :].rearrange("p m t -> p (m t)"), ACT.Copy).then_inc(m_ready, 1)

            def exp_piece(n):
                act.wait_ge(st_ps, n + 1)
                if n >= 2 * STP:
                    act.wait_ge(pv_ps, n // STP - 1)
                act.activation(pt[:, n % (2 * STP), :], ps[1 + n % 2][:, :], ACT.Exp).then_inc(exp_done, 1)

            for s in range(LAST_STEP + 1):
                for b in range(B):
                    if s == 2 * b + 6:
                        act.wait_ge(misc_ps, MISC["logits", b] + 1)
                        if b:
                            act.wait_ge(sel_ready, b)
                            act.wait_ge(e_ready, HT * b)
                        act.activation(lg[:, :, :].rearrange("p t e -> p (t e)"), misc[:, 0:HT * E],
                                       ACT.Copy).then_inc(misc_free, 1)
                if 3 <= s < NU + 3:
                    act.wait_ge(pv_ps, s - 2)
                    act.activation(yv[:, :, :].rearrange("p a t -> p (a t)"), bank(6), ACT.Copy)\
                        .then_inc(yv_ready, 1)
                if 2 <= s < NU + 2:
                    exp_piece(STP * (s - 2))
                for b in range(B):
                    if s == 2 * b + 6:
                        act.wait_ge(negm_ready, b + 1)
                        for t in range(HT):
                            act.activation(ee[:, t, :], lg[:, t, :], ACT.Exp,
                                           bias=negm[:, t:t + 1]).then_inc(e_ready, 1)
                if 1 <= s <= NU:
                    u = s - 1
                    act.wait_ge(misc_ps, MISC["negmax", u] + 1)
                    if u >= 2:
                        act.wait_ge(negrow_in[u % 2], 16 * (u // 2))
                    act.activation(nmt[:, u % 2, :], misc[0:2 * HG, 0:P].bitcast(BF16), ACT.Copy)\
                        .then_inc(misc_free, 1)
                if 2 <= s < NU + 2:
                    exp_piece(STP * (s - 2) + 1)
                    exp_piece(STP * (s - 2) + 2)
                if 3 <= s < NU + 3:
                    u = s - 3
                    act.wait_ge(yt_ps, u + 1)
                    if u >= 4:
                        act.wait_ge(misc_ps, MISC["proj", u // 2 - 2] + 1)
                    act.activation(y_t[:, u // 2 % 2, u % 2, :], bank(6)[:, 0:T], ACT.Copy).then_inc(yt_ready, 1)
                for b in range(B):
                    if s == 2 * b + 5:
                        act.wait_ge(misc_ps, MISC["xt", b] + 1)
                        act.activation(xt2[:, :, :].rearrange("p k t -> p (k t)"), misc[:, :],
                                       ACT.Copy).then_inc(misc_free, 1)

            act.wait_ge(slotc_ready, 1)
            for g in range(1, NG, 2):
                act.wait_ge(spread_ps, g + 1)
                if g > 1:
                    act.wait_ge(count_act, g // 2)
                act.activation(junk[:, 1, :], ps[SPREAD[g % 3]][:, :], ACT.Sign, bias=slot_c[:, 1:2], scale=-1.0,
                               accum_out=tok_n[:, g:g + 1]).then_inc(count_act, 1)

            for g in range(NG):
                act.wait_ge(up_ps, g + 1)
                if g:
                    act.wait_ge(hh_ready, g)
                act.activation(sil[:, :], bank(5)[:, 0:F], ACT.Silu).then_inc(sil_ready, 1)
                act.wait_ge(ht_ps, g + 1)
                if g >= 2:
                    act.wait_ge(down_ps, g - 1)
                act.activation(ht[:, g % 2, :], bank(6)[0:F, 0:P], ACT.Copy).then_inc(ht_ready, 1)
                act.wait_ge(down_ps, g + 1)
                act.wait_ge(gate_ready, g + 1)
                if g >= 2:
                    act.wait_ge(comb_ps, g - 1)
                act.activation(y3[:, g % 2, 0, :], bank(7)[:, 0:C], ACT.Copy,
                               scale=gate[:, g:g + 1]).then_inc(yh_ready, 1)

        @block.tensor
        def _(pe):
            def transpose_x(b):
                pe.wait_ge(xn_ready, HT * (b + 1))
                if b == 0:
                    pe.wait_ge(id_ready, 1)
                if b >= 2:
                    pe.wait_ge(xt_ready, b - 1)
                for t in range(HT):
                    for k in range(KC):
                        mm = pe.transpose(bank(b % 2)[:, k * T + t * P:k * T + (t + 1) * P],
                                          xn[:, b, t, k * P:(k + 1) * P], id32[:, :])
                mm.then_inc(xt_ps, 1)

            def qk(b):
                pe.wait_ge(xt_ready, b + 1)
                if b == 0:
                    pe.wait_ge(scaled, 2)
                if b >= 2:
                    pe.wait_ge(r_ready, 4 * (b - 1))
                for m in range(4):
                    for k in range(KC):
                        mm = pe.matmul(ps[1 + b % 2][:, m * T:(m + 1) * T], w_qk[:, k, m * P:(m + 1) * P],
                                       xnt[:, b % 2, k, :], start=(k == 0), stop=(k == KC - 1))
                mm.then_inc(qk_ps, 1)

            def v(b):
                if b == 0:
                    pe.wait_ge(wv_in, 16)
                if b >= 2:
                    pe.wait_ge(v_ready, HT * (b - 1))
                for t in range(HT):
                    for k in range(KC):
                        mm = pe.matmul(bank(6 + b % 2)[:, t * C:(t + 1) * C], xnt[:, b % 2, k, t * P:(t + 1) * P],
                                       w_v[:, k, :], start=(k == 0), stop=(k == KC - 1))
                mm.then_inc(v_ps, 1)

            pe.wait_ge(ones_ready, 1)
            for n in range(WARM_UP):
                pe.matmul(bank(7), ones[:, 0:P], ones[:, :], start=True, stop=True)
            transpose_x(0)
            for b in range(B):
                qk(b)
                if b + 1 < B:
                    transpose_x(b + 1)
                v(b)

            def scores(u, p):
                b, g, n = u // 2, u % 2, PIECES * u + p
                if n == 0:
                    pe.wait_ge(attn_const, ATTN_CONSTS)
                    pe.wait_ge(xt_ready, B)
                if p == 0 and g == 0:
                    pe.wait_ge(packed[b], 16 * N_PACK)
                if n >= 2:
                    pe.wait_ge(max_done, n - 1)
                nh, w, qt = (4, P, 0) if p < 2 else (2, T, 1)
                h0 = 4 * p if p < 2 else 2 * (p - 2)
                o = bank(p % 2).rearrange("q (h k) -> q h k", k=w)
                pe.matmul(o[:, :, w - P:w], id16[:, :], causal[:, :].unsqueeze(1).to_broadcast([P, nh, P]),
                          start=True, stop=False, skip_group_check=True)
                for h in range(nh):
                    mm = pe.matmul(o[:, h, :], q_of(b, g, h0 + h, qt * P, (qt + 1) * P, KP),
                                   k_of(b, g, h0 + h, 0, w, KP), start=False, stop=(h == nh - 1),
                                   skip_group_check=True)
                mm.then_inc(s_ps, 1)

            def negmax(u):
                pe.wait_ge(nmp_ready, u + 1)
                misc_wait("negmax", u)
                o = misc[0:2 * HG, 0:P].bitcast(BF16)
                for t in range(HT):
                    mm = pe.transpose(o[:, t * P:(t + 1) * P],
                                      nmp[:, u % 2, t, :, :].rearrange("p a h -> p (a h)"), id16[:, :])
                mm.then_inc(misc_ps, 1)

            def misc_wait(kind, n):
                if MISC[kind, n]:
                    pe.wait_ge(misc_free, MISC[kind, n])
                else:
                    pe.wait_ge(v_ready, HT * B)

            def scores_t(u, j):
                b, g, n = u // 2, u % 2, STP * u + j
                if j == 0:
                    pe.wait_ge(negrow_in[u % 2], 16 * (u // 2 + 1))
                if n == 0:
                    pe.wait_ge(r_ready, 4 * B)
                    pe.wait_ge(h_ready, 4 * B)
                if n >= 2:
                    pe.wait_ge(exp_done, n - 1)
                o = ps[1 + n % 2]
                if j < 2:
                    for h in range(4):
                        mm = pe.matmul(o[:, h * T:(h + 1) * T], k_of(b, g, 4 * j + h, 0, P, KP + 2),
                                       q_of(b, g, 4 * j + h, 0, T, KP + 2), start=True, stop=True)
                else:
                    for h in range(HG):
                        mm = pe.matmul(o[:, h * P:(h + 1) * P], k_of(b, g, h, P, T, KP + 2),
                                       q_of(b, g, h, P, T, KP + 2), start=True, stop=True)
                mm.then_inc(st_ps, 1)

            def pv(u):
                b, g = u // 2, u % 2
                pe.wait_ge(causal_done, STP * (u + 1))
                if u == 0:
                    pe.wait_ge(v_ready, HT * B)
                    pe.wait_ge(v_ones, B)
                else:
                    pe.wait_ge(yt_ready, u)
                for half in range(2):
                    for kt in range(HT):
                        for q in range(4):
                            h = 4 * half + q
                            buf = STP * u + (half if kt == 0 else 2)
                            n = T if kt == 0 else P
                            c0 = (q if kt == 0 else h) * n
                            mm = pe.matmul(bank(6)[32 * q:32 * q + 32, half * T + kt * P:(half + 1) * T],
                                           vz[:, kt * B + b, HG * g + h, :], pt[:, buf % (2 * STP), c0:c0 + n],
                                           start=(half == 0 and kt == 0), stop=(half == 1 and kt == 1),
                                           skip_group_check=True)
                mm.then_inc(pv_ps, 1)

            def queries_on_partitions(u):
                pe.wait_ge(yv_ready, u + 1)
                for t in range(HT):
                    for half in range(2):
                        mm = pe.transpose(bank(6)[:, t * T + half * P:t * T + (half + 1) * P],
                                          yv[:, half, t * P:(t + 1) * P], id32[:, :])
                mm.then_inc(yv_ps, 1)

            def dims_on_partitions(u):
                pe.wait_ge(yn_ready, u + 1)
                for t in range(HT):
                    mm = pe.transpose(bank(6)[:, t * P:(t + 1) * P],
                                      yn[:, t * HG:(t + 1) * HG, :].rearrange("p h d -> p (h d)"), id32[:, :])
                mm.then_inc(yt_ps, 1)

            def project(b):
                pe.wait_ge(yt_ready, 2 * b + 2)
                misc_wait("proj", b)
                for t in range(HT):
                    for k in range(KC):
                        mm = pe.matmul(misc[:, t * C:(t + 1) * C], y_t[:, b % 2, k, t * P:(t + 1) * P],
                                       w_proj[:, k, :], start=(k == 0), stop=(k == KC - 1))
                mm.then_inc(misc_ps, 1)

            def transpose_xn2(b):
                pe.wait_ge(xn2_ready, HT * (b + 1))
                misc_wait("xt", b)
                for t in range(HT):
                    for k in range(KC):
                        mm = pe.transpose(misc[:, k * T + t * P:k * T + (t + 1) * P],
                                          rows[:, t * B + b, k * P:(k + 1) * P], id32[:, :])
                mm.then_inc(misc_ps, 1)

            def logits(b):
                misc_wait("logits", b)
                for t in range(HT):
                    for k in range(KC):
                        mm = pe.matmul(misc[:, t * E:(t + 1) * E], xt2[:, k, t * P:(t + 1) * P], w_rt[:, k, :],
                                       start=(k == 0), stop=(k == KC - 1))
                mm.then_inc(misc_ps, 1)

            for s in range(LAST_STEP + 1):
                live = s < NU
                if live:
                    scores(s, 0)
                    scores(s, 1)
                for b in range(B):
                    if s == 2 * b + 6:
                        logits(b)
                    if s == 2 * b + 5:
                        project(b)
                if 3 <= s < NU + 3:
                    pv(s - 3)
                if 2 <= s < NU + 2:
                    scores_t(s - 2, 0)
                if 1 <= s <= NU:
                    negmax(s - 1)
                if live:
                    scores(s, 2)
                    scores(s, 3)
                if 3 <= s < NU + 3:
                    queries_on_partitions(s - 3)
                if 2 <= s < NU + 2:
                    scores_t(s - 2, 1)
                if live:
                    scores(s, 4)
                if 2 <= s < NU + 2:
                    scores_t(s - 2, 2)
                if 3 <= s < NU + 3:
                    dims_on_partitions(s - 3)
                if live:
                    scores(s, 5)
                for b in range(B):
                    if s == 2 * b + 5:
                        transpose_xn2(b)

            pe.wait_ge(sel_ready, B)
            pe.wait_ge(moe_const, MOE_CONSTS)
            pe.wait_ge(exp_done, STP * NU)
            for half in range(HT):
                srcs = [(t, ones[:, :]) for t in range(B * half)]
                srcs += [(half * B + b, before[:, 3 - b:7 - b, :].rearrange("p a t -> p (a t)")) for b in range(B)]
                for n, (t, r) in enumerate(srcs):
                    mm = pe.matmul(bank(2 + half)[0:E, :], sel[:, t, :], r, start=(n == 0), stop=(n == len(srcs) - 1))
                mm.then_inc(cum_ps, 1)
            pe.wait_ge(cumc_ready, HT)
            pe.wait_ge(misc_free, len(MISC))
            for g in range(NG):
                if g >= 3:
                    if (g - 3) % 2 == 0:
                        pe.wait_ge(count_dve, (g - 3) // 2 + 1)
                    else:
                        pe.wait_ge(count_act, (g - 3) // 2 + 1)
                for half in range(HT):
                    mm = pe.matmul(ps[SPREAD[g % 3]][:, half * 512:(half + 1) * 512], spread[:, g, :],
                                   cumc[:, half * 512:(half + 1) * 512], start=True, stop=True)
                mm.then_inc(spread_ps, 1)

            pe.wait_ge(count_dve, NG // 2)
            pe.wait_ge(count_act, NG // 2)

            def transpose_rows(g):
                pe.wait_ge(row_in[g % 4], 16 * (g // 4 + 1))
                if g:
                    pe.wait_ge(xg_ready, g)
                for k in range(KC):
                    mm = pe.transpose(bank(4)[:, k * P:(k + 1) * P], grow[:, g % 4, k * P:(k + 1) * P], id32[:, :])
                mm.then_inc(xg_ps, 1)

            def combine(g, n):
                if n == 0:
                    pe.wait_ge(hot_ready, g + 1)
                    pe.wait_ge(yh_ready, g + 1)
                elif n == 1:
                    pe.wait_ge(ym_ready, g + 1)
                else:
                    pe.wait_ge(yl_ready, g + 1)
                for t in range(NT):
                    mm = pe.matmul(bank(t // 2)[:, (t % 2) * C:(t % 2 + 1) * C], onehot[:, g % 2, t * P:(t + 1) * P],
                                   y3[:, g % 2, n, :], start=(g == 0 and n == 0 and t % 2 == 0),
                                   stop=(g == NG - 1 and n == 2), skip_group_check=True)
                    if n == 2 and (t == NT - 1 or (g == NG - 1 and t % 2)):
                        mm.then_inc(comb_ps, 1)

            transpose_rows(0)
            for g in range(NG + 1):
                if g < NG:
                    pe.wait_ge(xg_ready, g + 1)
                    pe.wait_ge(w13_in[g], 16)
                    if g:
                        pe.wait_ge(hh_ready, g)
                    for k in range(KC):
                        for q in range(EG):
                            mm = pe.matmul(bank(5)[q * CAP:(q + 1) * CAP, 0:2 * F],
                                           xgt[:, g % 2, k, q * CAP:(q + 1) * CAP], w13_sb[g][:, q, k, :],
                                           start=(k == 0), stop=(k == KC - 1))
                    mm.then_inc(up_ps, 1)
                if g:
                    combine(g - 1, 0)
                if g < NG:
                    pe.wait_ge(hh_ready, g + 1)
                    if g:
                        pe.wait_ge(ht_ready, g)
                    pe.transpose(bank(6)[0:F, 0:P], hh[:, :], id32[:, :]).then_inc(ht_ps, 1)
                if g:
                    combine(g - 1, 1)
                if g + 1 < NG:
                    transpose_rows(g + 1)
                if g < NG:
                    pe.wait_ge(ht_ready, g + 1)
                    pe.wait_ge(w2_in[g], 16)
                    if g:
                        pe.wait_ge(yr_ready, g)
                    for q in range(EG):
                        mm = pe.matmul(bank(7)[q * CAP:(q + 1) * CAP, 0:C], ht[:, g % 2, q * CAP:(q + 1) * CAP],
                                       w2_sb[g % W2S][:, q, :], start=True, stop=True)
                    mm.then_inc(down_ps, 1)
                if g:
                    combine(g - 1, 2)

        @block.vector
        def _(dve):
            steps = [0]

            def link(ins):
                steps[0] += 1
                ins.then_inc(dve_step, 1)
                dve.wait_ge(dve_step, steps[0])

            def moments(b):
                for t in range(HT):
                    ins = dve.bn_stats(stats[:, b, t, :], x_sb[:, t * B + b, :])
                    if t == HT - 1:
                        link(ins)
                for t in range(HT):
                    ins = dve.bn_aggr(mv[:, b, t, :], stats[:, b, t, :])
                    if t == HT - 1:
                        link(ins)
                return dve.tensor_scalar(ve[:, b, :], mv[:, b, :, 1], EPS, None, ALU.add)

            def moments1(b):
                dve.wait_ge(x_in[b], 16)
                moments(b).then_inc(var_ready, 1)

            def norm1(b):
                dve.wait_ge(rstd_ready, b + 1)
                for t in range(HT):
                    dve.tensor_scalar(xn[:, b, t, :], x_sb[:, t * B + b, :], mv[:, b, t, 0:1],
                                      rstd[:, b, t:t + 1], ALU.subtract, ALU.mult).then_inc(xn_ready, 1)

            dve.memset(ones[:, :], 1.0).then_inc(ones_ready, 1)
            moments1(0)
            dve.wait_ge(wqk_in, 16)
            dve.wait_ge(bqk_in, 16)
            dve.tensor_scalar(w_qk[:, :, 0:C], w_qk[:, :, 0:C], SCALE, None, ALU.mult).then_inc(scaled, 1)
            dve.tensor_scalar(b_qk[:, 0:2], b_qk[:, 0:2], SCALE, None, ALU.mult).then_inc(scaled, 1)
            norm1(0)
            moments1(1)
            moments1(2)
            norm1(1)
            norm1(2)
            for b in range(B):
                if b >= 2:
                    dve.wait_ge(l_ready, b - 1)
                for m in range(4):
                    dve.wait_ge(h_ready, 4 * b + 2 * (m // 2) + 2)
                    dve.scalar_tensor_tensor(out=res[:, b % 2, m, :], in0=ps[1 + b % 2][:, m * T:(m + 1) * T],
                                             scalar=b_qk[:, m:m + 1],
                                             in1=spl[:, b % 2, m // 2, (m % 2) * T:(m % 2 + 1) * T],
                                             op0=ALU.add, op1=ALU.subtract).then_inc(r_ready, 1)
                dve.wait_ge(v_ps, b + 1)
                if b == 0:
                    dve.wait_ge(small_in, N_SMALL)
                for t in range(HT):
                    dve.tensor_tensor(vz[:, t * B + b, :, 0:D],
                                      bank(6 + b % 2)[:, t * C:(t + 1) * C].rearrange("p (h d) -> p h d", d=D),
                                      b_v[:, :].rearrange("p (h d) -> p h d", d=D), ALU.add).then_inc(v_ready, 1)
                if b == 0:
                    moments1(3)
                    norm1(3)

            def row_max(u, p):
                n = PIECES * u + p
                dve.wait_ge(s_ps, n + 1)
                w, qt = (P, 0) if p < 2 else (T, 1)
                h0, nh = (4 * p, 4) if p < 2 else (2 * (p - 2), 2)
                dve.tensor_reduce(nm[:, u % 2, qt, h0:h0 + nh], bank(p % 2).rearrange("q (h k) -> q h k", k=w),
                                  AX.X, ALU.max, negate=True).then_inc(max_done, 1)

            def negmax_parts(u):
                dve.wait_ge(max_done, PIECES * (u + 1))
                if u >= 2:
                    dve.wait_ge(misc_ps, MISC["negmax", u - 2] + 1)
                link(dve.tensor_copy(nmp[:, u % 2, :, 0, :], nm[:, u % 2, :, :]))
                dve.tensor_tensor(nmp[:, u % 2, :, 1, :], nm[:, u % 2, :, :], nmp[:, u % 2, :, 0, :],
                                  ALU.subtract).then_inc(nmp_ready, 1)

            def over_sums(u):
                dve.wait_ge(yv_ps, u + 1)
                y = bank(6).rearrange("p (h a) -> p h a", a=2 * D)
                link(dve.reciprocal(rden[:, :].unsqueeze(2), y[:, :, D:D + 1]))
                dve.tensor_tensor(yn[:, :, :], y[:, :, 0:D], rden[:, :].unsqueeze(2).to_broadcast([P, HT * HG, D]),
                                  ALU.mult).then_inc(yn_ready, 1)

            def residual(b):
                dve.wait_ge(misc_ps, MISC["proj", b] + 1)
                dve.wait_ge(xb_ready, HT * (b + 1))
                dve.tensor_tensor(x_sb[:, b::B, :], misc.rearrange("p (t c) -> p t c", t=HT), x_sb[:, b::B, :],
                                  ALU.add).then_inc(misc_free, 1)
                dve.wait_ge(misc_free, MISC["proj", b] + 1)
                moments(b).then_inc(var2_ready, 1)

            def norm2(b):
                dve.wait_ge(rstd2_ready, b + 1)
                for t in range(HT):
                    dve.tensor_scalar(rows[:, t * B + b, 0:C], x_sb[:, t * B + b, :], mv[:, b, t, 0:1],
                                      rstd[:, b, t:t + 1], ALU.subtract, ALU.mult).then_inc(xn2_ready, 1)

            def choose(b):
                dve.wait_ge(misc_free, MISC["logits", b] + 1)
                for t in range(HT):
                    link(dve.max(m8[:, t, :], lg[:, t, :]))
                    link(dve.match_replace(lr[:, t, :], m8[:, t, :], lg[:, t, :], -3.0e38))
                if b:
                    dve.wait_ge(e_ready, HT * b)
                dve.tensor_scalar(negm[:, :], m8[:, 0:HT, 0], -1.0, None, ALU.mult).then_inc(negm_ready, 1)
                dve.tensor_tensor(sel[:, b::B, :], lr[:, :, :], lg[:, :, :], ALU.not_equal).then_inc(sel_ready, 1)

            def expert_weights(b):
                dve.wait_ge(e_ready, HT * (b + 1))
                dve.wait_ge(sel_ready, b + 1)
                link(dve.tensor_tensor(lr[:, :, :], ee[:, :, :], sel[:, b::B, :], ALU.mult))
                link(dve.tensor_reduce(wsum[:, :], lr[:, :, :], AX.X, ALU.add))
                link(dve.reciprocal(wrec[:, :], wsum[:, :]))
                for t in range(HT):
                    ins = dve.tensor_scalar(rows[:, t * B + b, C:ROW], lr[:, t, :], wrec[:, t:t + 1], None, ALU.mult)
                    if t == HT - 1:
                        ins.then_inc(rows_ready, 1)
                    else:
                        link(ins)

            for s in range(LAST_STEP + 1):
                live = s < NU
                if live:
                    row_max(s, 0)
                    row_max(s, 1)
                for b in range(B):
                    if s == 2 * b + 5:
                        residual(b)
                    if s == 2 * b + 6:
                        choose(b)
                if live:
                    row_max(s, 2)
                    row_max(s, 3)
                if 3 <= s < NU + 3:
                    over_sums(s - 3)
                for b in range(B):
                    if s == 2 * b + 5:
                        norm2(b)
                    if s == 2 * b + 6:
                        expert_weights(b)
                if live:
                    row_max(s, 4)
                    row_max(s, 5)
                    negmax_parts(s)

            dve.wait_ge(moe_const, MOE_CONSTS)
            link(dve.tensor_reduce(slot_c[:, 0:1], pc[:, :], AX.X, ALU.add))
            dve.tensor_scalar(slot_c[:, 1:2], slot_c[:, 0:1], 0.5, None, ALU.add).then_inc(slotc_ready, 1)
            dve.wait_ge(pv_ps, NU)
            for half in range(HT):
                dve.wait_ge(cum_ps, half + 1)
                dve.tensor_scalar(cumc[:, half * 512:(half + 1) * 512], bank(2 + half)[0:E, :], 2.0 * CAP, None,
                                  ALU.min).then_inc(cumc_ready, 1)
            for g in range(0, NG, 2):
                dve.wait_ge(spread_ps, g + 1)
                if g:
                    dve.wait_ge(count_dve, g // 2)
                dve.tensor_scalar(junk[:, 0, :], ps[SPREAD[g % 3]][:, :], slot_c[:, 0:1], 0.0, ALU.is_le, ALU.add,
                                  accum_out=tok_n[:, g:g + 1]).then_inc(count_dve, 1)
                if g % 4 == 2:
                    dve.wait_ge(count_act, g // 2 + 1)
                    dve.wait_ge(count_dve, g // 2 + 1)
                    odd = tok_n[:, g - 1:g + 2:2]
                    link(dve.tensor_scalar(odd, odd, 0.5, NTOK / 2, ALU.mult, ALU.add))
                    dve.tensor_scalar(tok_i[:, g - 2:g + 2], tok_n[:, g - 2:g + 2], NTOK - 1.0, None, ALU.min)\
                        .then_inc(tok_ready, 1)

            def take_rows(g):
                dve.wait_ge(row_in[g % 4], 16 * (g // 4 + 1))
                link(dve.tensor_tensor(g4[:, :], grow[:, g % 4, C + EG * g:C + EG * (g + 1)], eq4[:, :], ALU.mult))
                dve.tensor_reduce(gate[:, g:g + 1], g4[:, :], AX.X, ALU.add).then_inc(gate_ready, 1)
                dve.wait_ge(xg_ps, g + 1)
                if g >= 2:
                    dve.wait_ge(up_ps, g - 1)
                dve.tensor_copy(xgt[:, g % 2, :, :].rearrange("p k t -> p (k t)"), bank(4)[:, 0:KC * P])\
                    .then_inc(xg_ready, 1)

            take_rows(0)
            for g in range(NG):
                dve.wait_ge(sil_ready, g + 1)
                if g:
                    dve.wait_ge(ht_ps, g)
                dve.tensor_tensor(hh[:, :], bank(5)[:, F:2 * F], sil[:, :], ALU.mult).then_inc(hh_ready, 1)
                if g >= 2:
                    dve.wait_ge(comb_ps, g - 1)
                dve.tensor_scalar(onehot[:, g % 2, :], tokid[:, :], tok_n[:, g:g + 1], None, ALU.is_equal)\
                    .then_inc(hot_ready, 1)
                if g + 1 < NG:
                    take_rows(g + 1)
                dve.wait_ge(yh_ready, g + 1)
                dve.scalar_tensor_tensor(out=yr[:, :], in0=bank(7)[:, 0:C], scalar=gate[:, g:g + 1],
                                         in1=y3[:, g % 2, 0, :], op0=ALU.mult, op1=ALU.subtract)\
                    .then_inc(yr_ready, 1)
                dve.wait_ge(yr_ready, g + 1)
                dve.tensor_copy(y3[:, g % 2, 1, :], yr[:, :]).then_inc(ym_ready, 1)
                dve.wait_ge(ym_ready, g + 1)
                dve.tensor_tensor(y3[:, g % 2, 2, :], yr[:, :], y3[:, g % 2, 1, :], ALU.subtract)\
                    .then_inc(yl_ready, 1)
                dve.wait_ge(yl_ready, g + 1)
            for n in range(4):
                dve.wait_ge(comb_ps, NG + n)
                dve.tensor_tensor(x_sb[:, 2 * n:2 * n + 2, :], bank(n).rearrange("p (t c) -> p t c", t=2),
                                  x_sb[:, 2 * n:2 * n + 2, :], ALU.add).then_inc(fin_ready, 1)


_INS = ["x", "wqk", "bqk", "wv", "bv", "wproj", "bproj", "rwt", "w13", "w2"]


def kernel(L0_attn_x, L0_attn_w_attn, L0_attn_b_attn, L0_attn_w_proj, L0_attn_b_proj, L0_ffn_router_w, L0_ffn_w1,
           L0_ffn_v1, L0_ffn_w2):
    import numpy as np
    import concourse.bacc as bacc
    from concourse.bass_utils import run_bass_kernel_spmd

    def a(v):
        return np.ascontiguousarray(v)

    qk = np.asarray(L0_attn_w_attn)[:, :2 * C].reshape(C, 2, 2, HG, D).transpose(0, 1, 2, 4, 3).reshape(C, 2 * C)
    bqk = np.asarray(L0_attn_b_attn)[:2 * C].reshape(4, HG, D).transpose(2, 1, 0).reshape(P, 4)
    w1 = np.asarray(L0_ffn_w1).reshape(NG, EG, F, KC, P)
    v1 = np.asarray(L0_ffn_v1).reshape(NG, EG, F, KC, P)
    w13 = np.concatenate([w1, v1], axis=2).transpose(0, 4, 1, 3, 2)
    w2 = np.asarray(L0_ffn_w2).reshape(NG, EG, F, C).transpose(0, 2, 1, 3)
    host = {
        "x": a(L0_attn_x), "wqk": a(qk), "bqk": a(bqk), "wv": a(np.asarray(L0_attn_w_attn)[:, 2 * C:]),
        "bv": a(np.asarray(L0_attn_b_attn)[2 * C:]), "wproj": a(L0_attn_w_proj), "bproj": a(L0_attn_b_proj),
        "rwt": a(np.asarray(L0_ffn_router_w).T), "w13": a(w13), "w2": a(w2),
    }
    nc = bacc.Bacc("TRN2", target_bir_lowering=False, num_devices=1)
    args = [nc.dram_tensor(f"in_{n}", host[n].shape, mybir.dt.from_np(host[n].dtype), kind="ExternalInput").ap()
            for n in _INS]
    out = nc.dram_tensor("out_0", (B, T, C), F32, kind="ExternalOutput").ap()
    build(nc, *args, out)
    r = run_bass_kernel_spmd(nc, [{f"in_{n}": host[n] for n in _INS}], core_ids=[0])
    return r.results[0]["out_0"]
```

```python
from contextlib import ExitStack

import concourse.bass as bass
from concourse import mybir

F32 = mybir.dt.float32
BF16 = mybir.dt.bfloat16
F16 = mybir.dt.float16
U32 = mybir.dt.uint32
ALU = mybir.AluOpType
ACT = mybir.ActivationFunctionType
AX = mybir.AxisListType

P = 128
B, T, C = 4, 256, 256
H, D = 16, 16
E, TOPK, F, CAP = 64, 8, 96, 32
KC = C // P
HT = T // P
NT = B * HT
HG = 8
NU = B * H // HG
PARTS = [(0, 0), (0, 1), (1, 0), (1, 1), (0, 2), (2, 0)]
KP = D * len(PARTS)
EPS = 1e-5
SCALE = D ** -0.5
MASKED = -1e30
EG = P // CAP
NG = E // EG
ROW = C + E
NTOK = B * T
TS = P // B
FINISH = [2, 3, 1, 0]
APART = 1
W2S = 9
PIECES = 6
STP = 3
EARLY = {2: 1, 3: 1}
WARM_UP = 11
BATCH = {"project": lambda s: (s - 4) // 2 if s % 2 == 0 and s >= 4 else None,
         "router": lambda s: (s - 5) // 2 if s % 2 and s >= 5 else None,
         "weights": lambda s: (s - 6) // 2 if s % 2 == 0 and s >= 6 else None}
N_PACK = 1 + len(PARTS) + sum(pq > pk for pq, pk in PARTS)
ATTN_CONSTS = 2
MOE_CONSTS = 4 + NT // 2 + NG // 2
ALWAYS = 3
MORE = 4
AHEAD = 4


def misc_schedule():
    order = []
    for s in range(NU):
        if s:
            order.append(("negmax", s - 1))
        if BATCH["router"](s) is not None:
            order += [("xt", BATCH["router"](s)), ("logits", BATCH["router"](s))]
        if BATCH["project"](s) is not None:
            order.append(("proj", BATCH["project"](s)))
    order += [("negmax", NU - 1), ("proj", B - 2), ("xt", B - 2), ("logits", B - 2), ("proj", B - 1), ("xt", B - 1),
              ("logits", B - 1)]
    return {use: n for n, use in enumerate(order)}


def build(nc, x, wqk, bqk, wv, bv, wproj, bproj, rwt, w13, w2, out):
    with ExitStack() as ctx:
        ent = ctx.enter_context

        def sb(name, shape, dt):
            return ent(nc.sbuf_tensor(name, shape, dt))

        def sem(name):
            return ent(nc.semaphore(name))

        x_sb = sb("x_sb", [P, NT, C], F32)
        id32 = sb("id32", [P, P], F32)
        id16 = sb("id16", [P, P], BF16)
        causal = sb("causal", [P, P], BF16)
        before = sb("before", [P, 7, P], BF16)
        ones = sb("ones", [P, 4 * P], BF16)
        zero16 = sb("zero16", [P, P], BF16)
        need = sb("need", [E, 1], F32)
        need_at = sb("need_at", [E, HT * B], F32)
        digit = sb("digit", [1, 2, NG // 2], F32)
        past = sb("past", [1, 2, 2, NG // 2], F32)
        reach_f = sb("reach_f", [1, 2], F32)
        reach_i = sb("reach_i", [1, 2], U32)
        spread = sb("spread", [E, NG, P], BF16)
        tokid = sb("tokid", [P, NTOK], F16)
        w_proj = sb("w_proj", [P, KC, C], F32)
        w_rt = sb("w_rt", [P, KC, E], F32)
        b_v = sb("b_v", [P, C], F32)
        b_proj = sb("b_proj", [P, C], F32)
        b_qk = sb("b_qk", [P, 4], F32)
        stats = sb("stats", [P, B, HT, 6], F32)
        mv = sb("mv", [P, B, HT, 2], F32)
        ve = sb("ve", [P, B, HT], F32)
        rstd = sb("rstd", [P, B, HT], F32)
        mhalf = sb("mhalf", [P, HT], F32)
        sel = sb("sel", [P, NT, E], BF16)
        slot_c = sb("slot_c", [P, 2], F32)
        pc = sb("pc", [P, EG], F32)
        eq4 = sb("eq4", [P, EG], F32)
        cnt = sb("cnt", [P, HT, NG], F32)
        tok_n = sb("tok_n", [P, NG], F32)
        tok_i = sb("tok_i", [P, NG], U32)
        m8 = sb("m8", [P, HT, TOPK], F32)
        e8 = sb("e8", [P, HT, TOPK], F32)
        negm = sb("negm", [P, HT], F32)
        wsum = sb("wsum", [P, HT], F32)
        wrec = sb("wrec", [P, HT], F32)
        lg = sb("lg", [P, HT, E], F32)
        lr = sb("lr", [P, HT, E], F32)
        ee = sb("ee", [P, HT, E], F32)
        nm = sb("nm", [P, 2, HT, HG], F32)
        nmp = sb("nmp", [P, 2, HT, 2, HG], BF16)
        nmt = sb("nmt", [2 * HG, 2, T], BF16)
        y_t = sb("y_t", [P, 2, KC, T], F32)
        yv = sb("yv", [P, 2, T], F32)
        rden = sb("rden", [P, HT * HG], F32)
        yn = sb("yn", [P, HT * HG, D], F32)
        xt2 = sb("xt2", [P, KC, T], F32)

        size = {F32: 4, BF16: 2, F16: 2}
        at = [(nc.sbuf_base + 31) // 32 * 32]
        words = (nc.sbuf_bytes_remaining - 256) // 4
        top = at[0] + 4 * words - 64
        sb("arena", [P, words], F32)

        def place(name, shape, dt, offset=None):
            n = size[dt]
            for d in shape[1:]:
                n *= d
            n = (n + 31) // 32 * 32
            if offset is None:
                offset = at[0]
                at[0] += n
                assert at[0] <= top, (name, at[0], top)
            return nc.alloc_sbuf_tensor_at(name, shape, dt, offset=offset)

        rows_at = at[0]
        rows = place("rows", [P, NT, ROW], F32)
        x_tok = nc.alloc_sbuf_tensor_at("x_tok", [P, NT, C], F32, offset=rows_at)

        W13B, W2B = EG * KC * 2 * F * 4, EG * C * 4
        w13_at, w2_at = {}, {}
        pack, pack_at = [], []
        for b in range(B):
            pack_at.append(at[0])
            pack.append(place(f"pack{b}", [KP + 2, HG, 2, 2, T], BF16))
            w13_at[8 + 2 * b] = pack_at[b]
            w13_at[9 + 2 * b] = pack_at[b] + W13B
            w2_at[1 + b] = pack_at[b] + 2 * W13B
        vz_at = at[0]
        vz = place("vz", [P, NT, H, 32], F32)
        for n in range(4):
            w2_at[5 + n] = vz_at + n * W2B
        pt_at = at[0]
        pt = place("pt", [P, 2 * STP, 1024], F32)
        xn = nc.alloc_sbuf_tensor_at("xn", [P, B, HT, C], F32, offset=pt_at)
        a_at = at[0]
        w_qk = place("w_qk", [P, KC, 2 * C], F32)
        w_v = place("w_v", [P, KC, C], F32)
        xnt = place("xnt", [P, 2, KC, T], F32)
        spl = place("spl", [P, 2, 3 * 2, 2 * T], BF16)
        res = place("res", [P, 2, 4, T], F32)
        a_end = at[0] = max(at[0], a_at + 5 * W13B + W2B)
        free_chunks = min(3, (top - a_end) // W13B)
        for n in range(5):
            w13_at[free_chunks + n] = a_at + n * W13B
        w2_at[0] = a_at + 5 * W13B
        for n in range(free_chunks):
            w13_at[n] = a_end + n * W13B
        assert free_chunks == 3
        w13_sb = [nc.alloc_sbuf_tensor_at(f"w13_{g}", [P, EG, KC, 2 * F], F32, offset=w13_at[g]) for g in range(NG)]
        w2_sb = [nc.alloc_sbuf_tensor_at(f"w2_{g}", [F, EG, C], F32, offset=w2_at[g]) for g in range(W2S)]
        d_at = at[0]
        at[0] = pt_at
        cumc = place("cumc", [E, NTOK], BF16)
        junk = place("junk", [P, HT, NTOK // 2], BF16)
        onehot = place("onehot", [P, 2, NTOK], BF16)
        grow = place("grow", [P, 4, ROW], F32)
        xgt = place("xgt", [P, 2, KC, P], F32)
        sil = place("sil", [P, F], F32)
        hh = place("hh", [P, F], F32)
        ht = place("ht", [F, 2, P], F32)
        y3 = place("y3", [P, 2, 3, C], BF16)
        yr = place("yr", [P, C], F32)
        g4 = place("g4", [P, EG], F32)
        gate = place("gate", [P, NG], F32)
        assert at[0] <= a_at
        at[0] = d_at

        xrow = nc.dram_tensor("xrow", [NTOK, ROW], F32, kind="Internal").ap()

        ps = [ent(nc.psum_tensor(f"pair{n}", [P, 1024], F32)) for n in range(4)]

        def bank(n):
            return ps[n // 2][:, (n % 2) * 512:(n % 2) * 512 + 512]

        x_in = [sem(f"x_in{b}") for b in range(B)]
        wqk_in, wv_in, bqk_in, small_in = sem("wqk_in"), sem("wv_in"), sem("bqk_in"), sem("small_in")
        scaled = sem("scaled")
        ones_ready, slotc_ready = sem("ones_ready"), sem("slotc_ready")
        v_ones, id_ready, attn_const, moe_const = sem("v_ones"), sem("id_ready"), sem("attn_const"), sem("moe_const")
        var_ready, rstd_ready, xn_ready = sem("var_ready"), sem("rstd_ready"), sem("xn_ready")
        xt_ps, xt_ready = sem("xt_ps"), sem("xt_ready")
        qk_ps, v_ps = sem("qk_ps"), sem("v_ps")
        h_ready, r_ready, m_ready, l_ready, v_ready = (sem("h_ready"), sem("r_ready"), sem("m_ready"),
                                                       sem("l_ready"), sem("v_ready"))
        packed = [sem(f"packed{b}") for b in range(B)]
        xb_ready = sem("xb_ready")
        s_ps, max_done = sem("s_ps"), sem("max_done")
        nmp_ready = sem("nmp_ready")
        negrow_in = [sem(f"negrow_in{n}") for n in range(2)]
        st_ps, exp_done, causal_done = sem("st_ps"), sem("exp_done"), sem("causal_done")
        pv_ps, yv_ready, yv_ps, yn_ready, yt_ps, yt_ready = (sem("pv_ps"), sem("yv_ready"), sem("yv_ps"),
                                                             sem("yn_ready"), sem("yt_ps"), sem("yt_ready"))
        misc_ps, misc_free = sem("misc_ps"), sem("misc_free")
        var2_ready, rstd2_ready, xn2_ready = sem("var2_ready"), sem("rstd2_ready"), sem("xn2_ready")
        negm_ready, e_ready, sel_ready, rows_ready = (sem("negm_ready"), sem("e_ready"), sem("sel_ready"),
                                                      sem("rows_ready"))
        rows_out = [sem(f"rows_out{b}") for b in range(B)]
        need_ready, need_ps, need_in, x_tok_in, zero_ready = (sem("need_ready"), sem("need_ps"), sem("need_in"),
                                                              sem("x_tok_in"), sem("zero_ready"))
        cum_ps, cumc_dve, cumc_act = sem("cum_ps"), sem("cumc_dve"), sem("cumc_act")
        spread_ps, count_dve, count_act, tok_ready = (sem("spread_ps"), sem("count_dve"), sem("count_act"),
                                                      sem("tok_ready"))
        row_in = [sem(f"row_in{n}") for n in range(4)]
        w13_in = [sem(f"w13_in{g}") for g in range(NG)]
        w2_in = [sem(f"w2_in{g}") for g in range(NG)]
        xg_ps, xg_ready, gate_ready = sem("xg_ps"), sem("xg_ready"), sem("gate_ready")
        up_ps, sil_ready, hh_ready = sem("up_ps"), sem("sil_ready"), sem("hh_ready")
        ht_ps, ht_ready, down_ps = sem("ht_ps"), sem("ht_ready"), sem("down_ps")
        yh_ready, yr_ready, ym_ready, yl_ready = sem("yh_ready"), sem("yr_ready"), sem("ym_ready"), sem("yl_ready")
        tokn_ready = sem("tokn_ready")
        hot_ready, comb_ps, fin_ready, out_done = sem("hot_ready"), sem("comb_ps"), sem("fin_ready"), sem("out_done")
        dve_step = sem("dve_step")
        pool_step = sem("pool_step")

        MISC = misc_schedule()
        misc = bank(7)
        up_bank, down_bank = bank(4), bank(5)

        def pv_bank(u):
            return bank(6 if u < NU - 1 else 0)

        def rank_bank(g, half):
            return bank((2 if g < AHEAD and g % 2 else 6) + half)

        N_SMALL = 4 * 16
        q_of = lambda b, g, h, lo, hi, k: pack[b][0:k, h, 0, g, lo:hi]
        k_of = lambda b, g, h, lo, hi, k: pack[b][0:k, h, 1, g, lo:hi]

        block = ent(nc.Block())

        @block.sync
        def _(sp):
            def load_w13(g):
                sp.dma_start(w13_sb[g][:, :, :, :], w13[g]).then_inc(w13_in[g], 16)

            def load_x_tok(batches):
                for b in batches:
                    for k in range(NT):
                        half, first, step = k // (NT // HT), 2 * TS * (k // 2) % P + k % 2, 2
                        if k // 2 == APART:
                            first, step = TS * k % P, 1
                        sp.dma_start(x_tok[b::B, k, :],
                                     x_sb[first:first + step * (TS - 1) + 1:step, half * B + b, :])\
                            .then_inc(x_tok_in, 16)

            def load_w2(g):
                sp.dma_start(w2_sb[g % W2S][:, :, :], w2[g]).then_inc(w2_in[g], 16)

            def load_x(b):
                sp.dma_start(x_sb[:, b::B, :], x[b].rearrange("(h p) c -> p h c", p=P)).then_inc(x_in[b], 16)

            load_x(0)
            sp.dma_start(w_qk[:, :, :], wqk.rearrange("(k p) n -> p k n", p=P)).then_inc(wqk_in, 16)
            sp.dma_start(b_qk[:, :], bqk).then_inc(bqk_in, 16)
            load_x(1)
            sp.dma_start(w_v[:, :, :], wv.rearrange("(k p) n -> p k n", p=P)).then_inc(wv_in, 16)
            sp.dma_start(b_v[:, :], bv.partition_broadcast(P)).then_inc(small_in, 16)
            sp.dma_start(b_proj[:, :], bproj.partition_broadcast(P)).then_inc(small_in, 16)
            load_x(2)
            load_x(3)
            sp.dma_start(w_proj[:, :, :], wproj.rearrange("(k p) n -> p k n", p=P)).then_inc(small_in, 16)
            sp.dma_start(w_rt[:, :, :], rwt.rearrange("(k p) n -> p k n", p=P)).then_inc(small_in, 16)
            sp.wait_ge(ones_ready, 1)
            for b in range(B):
                sp.dma_start(pack[b][KP:KP + 2, :, 1, :, :].rearrange("r h g t -> r h (g t)"),
                             ones[0:2 * HG, :]).then_inc(packed[b], 16)
            for g in range(3):
                load_w13(g)
            for b in range(B):
                pair = spl[:, b % 2, :, :]
                for n, (pq, pk) in enumerate(PARTS):
                    if n == 0:
                        sp.wait_ge(h_ready, 4 * (b + 1))
                    if n == 1:
                        sp.wait_ge(m_ready, b + 1)
                    if n == 4:
                        sp.wait_ge(l_ready, b + 1)
                    dst = pack[b][n * D:(n + 1) * D, :, :, :, :]
                    iq, ik = 2 * pq, 2 * pk + 1
                    if ik > iq:
                        sp.dma_start(dst.rearrange("d h a g t -> d h (a g t)"),
                                     pair[:, iq:ik + 1:ik - iq, :]).then_inc(packed[b], 16)
                    else:
                        sp.dma_start(dst[:, :, 0, :, :].rearrange("d h g t -> d h (g t)"),
                                     pair[:, iq, :]).then_inc(packed[b], 16)
                        sp.dma_start(dst[:, :, 1, :, :].rearrange("d h g t -> d h (g t)"),
                                     pair[:, ik, :]).then_inc(packed[b], 16)
            late = list(range(3, 8))
            for s in range(1, 2 * B + 6):
                if s <= NU:
                    u = s - 1
                    sp.wait_ge(misc_free, MISC["negmax", u] + 1)
                    sp.dma_start(pack[u // 2][KP:KP + 2, :, 0, u % 2, :], nmt[:, u % 2, :])\
                      .then_inc(negrow_in[u % 2], 16)
                if s == 1:
                    for b in range(B):
                        sp.wait_ge(packed[b], 16 * N_PACK)
                    sp.wait_ge(l_ready, B)
                    sp.wait_ge(v_ready, HT * B)
                if late:
                    load_w13(late.pop(0))
                    if not late:
                        load_w2(0)
                for b in range(B):
                    if s == 2 * b + 4:
                        sp.wait_ge(st_ps, STP * (2 * b + 2))
                        load_w13(8 + 2 * b)
                        load_w13(9 + 2 * b)
                        load_w2(1 + b)
                    if s == 2 * b + 7:
                        xrow_b = xrow.rearrange("(h s b) c -> b s h c", b=B, h=HT)[b]
                        parts = ([(rows_ready, 0, ROW)] if b < B - 1 else
                                 [(xn2_ready, 0, C), (rows_ready, C, ROW)])
                        for written, c0, c1 in parts:
                            sp.wait_ge(written, HT * (b + 1))
                            sp.dma_start(xrow_b[:, :, c0:c1], rows[:, b::B, c0:c1]).then_inc(rows_out[b], 16)
                if s == 2 * B + 4:
                    sp.wait_ge(pv_ps, NU)
                    for n in range(5, W2S):
                        load_w2(n)
            for b in range(B):
                sp.wait_ge(rows_out[b], 32 if b == B - 1 else 16)
            load_x_tok(range(1))
            for g in range(W2S, NG):
                sp.wait_ge(down_ps, g - W2S + 1)
                load_w2(g)
                load_x_tok(range(g - W2S + 1, min(g - W2S + 2, B)))
            for n, pair in enumerate(FINISH):
                sp.wait_ge(fin_ready, n + 1)
                out_rows = out[:, 2 * TS * pair:2 * TS * (pair + 1), :]
                if pair == APART:
                    for j in range(2):
                        sp.dma_start(out_rows[:, TS * j:TS * (j + 1), :].rearrange("b s c -> s b c"),
                                     x_tok[:, 2 * pair + j, :]).then_inc(out_done, 16)
                else:
                    sp.dma_start(out_rows.rearrange("b (s j) c -> s b (j c)", j=2),
                                 x_tok[:, 2 * pair:2 * pair + 2, :].rearrange("p j c -> p (j c)")).then_inc(out_done, 16)
            sp.wait_ge(out_done, 16 * (NT // 2 + 1))

        @block.gpsimd
        def _(pool):
            steps = [0]

            def link(ins):
                steps[0] += 1
                ins.then_inc(pool_step, 1)
                pool.wait_ge(pool_step, steps[0])

            link(pool.memset(id32[:, :], 0.0))
            pool.affine_select(out=id32[:, :], in_=id32[:, :], compare_op=ALU.not_equal, fill=1.0, base=0,
                               pattern=[[-1, P]], channel_multiplier=1).then_inc(id_ready, 1)
            link(pool.memset(mhalf[:, :], -0.5))

            def pow_rstd(b, ready, done):
                pool.wait_ge(ready, b + 1)
                pool.tensor_tensor(out=rstd[:, b, :], in0=ve[:, b, :], in1=mhalf[:, :],
                                   op=ALU.pow).then_inc(done, 1)

            for b in range(B - 1):
                pow_rstd(b, var_ready, rstd_ready)
                if b == 0:
                    pool.memset(vz[:, 0::B, :, D:], 1.0).then_inc(v_ones, 1)
            for b in range(B):
                pool.wait_ge(m_ready, b + 1)
                if b >= 2:
                    pool.wait_ge(packed[b - 2], 16 * N_PACK)
                pool.tensor_tensor(out=spl[:, b % 2, 4:6, :].rearrange("p a n -> p (a n)"),
                                   in0=res[:, b % 2, :, :].rearrange("p m t -> p (m t)"),
                                   in1=spl[:, b % 2, 2:4, :].rearrange("p a n -> p (a n)"),
                                   op=ALU.subtract).then_inc(l_ready, 1)
                if b == 0:
                    pow_rstd(B - 1, var_ready, rstd_ready)
                    for n in range(1, B):
                        pool.memset(vz[:, n::B, :, D:], 1.0).then_inc(v_ones, 1)
                pool.wait_ge(xn_ready, HT * (b + 1))
                if b == 0:
                    pool.wait_ge(small_in, N_SMALL)
                for t in range(HT):
                    pool.tensor_tensor(out=x_sb[:, t * B + b, :], in0=x_sb[:, t * B + b, :], in1=b_proj[:, :],
                                       op=ALU.add).then_inc(xb_ready, 1)
                if b == 1:
                    link(pool.memset(id16[:, :], 0.0))
                    pool.affine_select(out=id16[:, :], in_=id16[:, :], compare_op=ALU.not_equal, fill=1.0, base=0,
                                       pattern=[[-1, P]], channel_multiplier=1).then_inc(attn_const, 1)
                    link(pool.memset(causal[:, :], 0.0))
                    pool.affine_select(out=causal[:, :], in_=causal[:, :], compare_op=ALU.is_ge, fill=MASKED, base=0,
                                       pattern=[[-1, P]], channel_multiplier=1).then_inc(attn_const, 1)
            def causal_zero(n):
                pool.wait_ge(exp_done, n + 1)
                buf, j = n % (2 * STP), n % STP
                v = pt[:, buf, :].rearrange("p (h t) -> p h t", t=T if j < 2 else P)[:, :, 0:P]
                pool.affine_select(out=v, in_=v, compare_op=ALU.is_ge, fill=0.0, base=0,
                                   pattern=[[0, 4 if j < 2 else 8], [1, P]], channel_multiplier=-1)\
                    .then_inc(causal_done, 1)

            def moe_consts(part):
                if part == 0:
                    link(pool.memset(before[:, :, :], 1.0))
                    pool.affine_select(out=before[:, 0:3, :], in_=before[:, 0:3, :], compare_op=ALU.is_gt, fill=0.0,
                                       base=0, pattern=[[0, 3], [1, P]], channel_multiplier=-1).then_inc(moe_const, 1)
                    pool.affine_select(out=before[:, 3:7, :], in_=before[:, 3:7, :], compare_op=ALU.is_ge, fill=0.0,
                                       base=0, pattern=[[0, 4], [1, P]], channel_multiplier=-1).then_inc(moe_const, 1)
                elif part == 1:
                    link(pool.memset(spread[:, :, :], 0.0))
                elif part == 2:
                    pool.affine_select(out=spread[:, :, :].rearrange("e g (q c) -> e g q c", q=EG),
                                       in_=spread[:, :, :].rearrange("e g (q c) -> e g q c", q=EG),
                                       compare_op=ALU.not_equal, fill=1.0, base=0,
                                       pattern=[[-EG, NG], [-1, EG], [0, CAP]], channel_multiplier=1)\
                        .then_inc(moe_const, 1)
                elif part == 3:
                    for pair in range(NT // 2):
                        tile, step = (TS * B, B) if pair == APART else (B, 2 * B)
                        pool.iota(tokid[:, 2 * P * pair:2 * P * (pair + 1)].rearrange("p (j s b) -> p j s b", j=2, b=B),
                                  pattern=[[tile, 2], [step, TS], [1, B]], base=2 * P * pair, channel_multiplier=0,
                                  allow_small_or_imprecise_dtypes=True).then_inc(moe_const, 1)
                elif part == 4:
                    pool.memset(zero16[:, :], 0.0).then_inc(zero_ready, 1)
                    for n in range(NG // 2):
                        pool.memset(digit[:, :, n], 4.0 ** n).then_inc(moe_const, 1)
                    link(pool.memset(eq4[:, :], 1.0))
                    link(pool.affine_select(out=eq4[:, :], in_=eq4[:, :], compare_op=ALU.is_ge, fill=0.0, base=0,
                                            pattern=[[-CAP, EG]], channel_multiplier=1))
                    link(pool.affine_select(out=eq4[:, :], in_=eq4[:, :], compare_op=ALU.is_ge, fill=0.0,
                                            base=CAP - 1, pattern=[[CAP, EG]], channel_multiplier=-1))
                    link(pool.iota(pc[:, :], pattern=[[-CAP, EG]], base=0, channel_multiplier=1,
                                   allow_small_or_imprecise_dtypes=True))
                    pool.tensor_tensor(out=pc[:, :], in0=pc[:, :], in1=eq4[:, :], op=ALU.mult)\
                        .then_inc(moe_const, 1)

            for s in range(1, NU):
                if s == 2:
                    causal_zero(0)
                if s >= 2:
                    causal_zero(STP * (s - 2) + 1)
                    causal_zero(STP * (s - 2) + 2)
                if s > 1:
                    causal_zero(STP * (s - 1))
                if BATCH["project"](s) is not None:
                    pow_rstd(BATCH["project"](s), var2_ready, rstd2_ready)
                if s >= 3:
                    moe_consts(s - 3)
            for n in range(STP * (NU - 2) + 1, STP * NU):
                causal_zero(n)
            pow_rstd(B - 2, var2_ready, rstd2_ready)
            pow_rstd(B - 1, var2_ready, rstd2_ready)

            def gather(g):
                if g % 2 == 0:
                    pool.wait_ge(tok_ready, g // 2 + 1)
                if g == 0:
                    for b in range(B):
                        pool.wait_ge(rows_out[b], 32 if b == B - 1 else 16)
                if g >= 4:
                    pool.wait_ge(xg_ps, g - 3)
                    pool.wait_ge(gate_ready, g - 3)
                pool.indirect_dma_start(out=grow[:, g % 4, :], out_offset=None, in_=xrow,
                                        in_offset=bass.IndirectOffsetOnAxis(ap=tok_i[:, g:g + 1], axis=0))\
                    .then_inc(row_in[g % 4], 16)

            def later_tokens(g):
                pool.wait_ge(count_act, g + 2)
                pool.tensor_scalar(tok_n[:, g:g + 2], cnt[:, 1, g:g + 2], 0.5, NTOK / 2, ALU.mult, ALU.add)\
                    .then_inc(tokn_ready, 1)
                pool.wait_ge(tokn_ready, g // 2 + 1)
                pool.tensor_scalar(tok_i[:, g:g + 2], tok_n[:, g:g + 2], NTOK - 1.0, None, ALU.min)\
                    .then_inc(tok_ready, 1)

            for g in range(NG):
                if g >= AHEAD and g % 2 == 0:
                    later_tokens(g)
                gather(g)

        @block.scalar
        def _(act):
            def copy_xt(b):
                act.wait_ge(xt_ps, b + 1)
                if b >= 2:
                    act.wait_ge(v_ps, b - 1)
                act.activation(xnt[:, b % 2, :, :].rearrange("p k t -> p (k t)"), bank(b % 2),
                               ACT.Copy).then_inc(xt_ready, 1)

            copy_xt(0)
            act.wait_ge(scaled, 2)
            for b in range(B):
                act.wait_ge(qk_ps, b + 1)
                if b >= 2:
                    act.wait_ge(packed[b - 2], 16 * N_PACK)
                for m in range(4):
                    act.activation(spl[:, b % 2, m // 2, (m % 2) * T:(m % 2 + 1) * T],
                                   ps[1 + b % 2][:, m * T:(m + 1) * T], ACT.Identity,
                                   bias=b_qk[:, m:m + 1]).then_inc(h_ready, 1)
                if b + 1 < B:
                    copy_xt(b + 1)
                act.wait_ge(r_ready, 4 * (b + 1))
                act.activation(spl[:, b % 2, 2:4, :].rearrange("p a n -> p (a n)"),
                               res[:, b % 2, :, :].rearrange("p m t -> p (m t)"), ACT.Copy).then_inc(m_ready, 1)

            def exp_piece(n):
                act.wait_ge(st_ps, n + 1)
                if n >= 2 * STP:
                    act.wait_ge(pv_ps, n // STP - 1)
                act.activation(pt[:, n % (2 * STP), :], ps[1 + n % 2][:, :], ACT.Exp).then_inc(exp_done, 1)

            def copy_negmax(u):
                act.wait_ge(misc_ps, MISC["negmax", u] + 1)
                if u >= 2:
                    act.wait_ge(negrow_in[u % 2], 16 * (u // 2))
                act.activation(nmt[:, u % 2, :], misc[0:2 * HG, 0:P].bitcast(BF16), ACT.Copy).then_inc(misc_free, 1)

            def copy_yv(u):
                act.wait_ge(pv_ps, u + 1)
                if u:
                    act.wait_ge(yv_ps, u)
                act.activation(yv[:, :, :].rearrange("p a t -> p (a t)"), pv_bank(u), ACT.Copy).then_inc(yv_ready, 1)

            def copy_yt(u):
                act.wait_ge(yt_ps, u + 1)
                if u >= 4:
                    act.wait_ge(misc_ps, MISC["proj", u // 2 - 2] + 1)
                act.activation(y_t[:, u // 2 % 2, u % 2, :], pv_bank(u)[:, 0:T], ACT.Copy).then_inc(yt_ready, 1)

            def copy_xn2(b):
                act.wait_ge(misc_ps, MISC["xt", b] + 1)
                act.activation(xt2[:, :, :].rearrange("p k t -> p (k t)"), misc[:, :], ACT.Copy).then_inc(misc_free, 1)

            def copy_logits(b):
                act.wait_ge(misc_ps, MISC["logits", b] + 1)
                if b:
                    act.wait_ge(sel_ready, b)
                    act.wait_ge(e_ready, 2 * HT * b)
                act.activation(lg[:, :, :].rearrange("p t e -> p (t e)"), misc[:, 0:HT * E],
                               ACT.Copy).then_inc(misc_free, 1)

            def router_exps(b):
                act.wait_ge(negm_ready, b + 1)
                if b:
                    act.wait_ge(rows_ready, HT * b)
                for t in range(HT):
                    act.activation(e8[:, t, :], m8[:, t, :], ACT.Exp, bias=negm[:, t:t + 1],
                                   accum_out=wsum[:, t:t + 1]).then_inc(e_ready, 1)
                    act.activation(ee[:, t, :], lg[:, t, :], ACT.Exp, bias=negm[:, t:t + 1]).then_inc(e_ready, 1)

            for s in range(1, NU):
                router = BATCH["router"](s)
                copy_negmax(s - 1)
                if s == 2:
                    exp_piece(0)
                if s >= 2:
                    exp_piece(STP * (s - 2) + 1)
                if s >= 3:
                    copy_yt(s - 3)
                if s >= 2:
                    exp_piece(STP * (s - 2) + 2)
                if router is not None:
                    copy_xn2(router)
                if s > 1:
                    exp_piece(STP * (s - 1))
                if router is not None:
                    copy_logits(router)
                if s == NU - 1:
                    copy_negmax(NU - 1)
                if s >= 2:
                    copy_yv(s - 2)
                if router is not None and s < NU - 1:
                    router_exps(router)
            exp_piece(STP * (NU - 2) + 1)
            exp_piece(STP * (NU - 2) + 2)
            copy_yt(NU - 3)
            exp_piece(STP * (NU - 1))
            exp_piece(STP * (NU - 1) + 1)
            exp_piece(STP * (NU - 1) + 2)
            router_exps(B - 3)
            copy_yv(NU - 2)
            copy_yv(NU - 1)
            copy_xn2(B - 2)
            copy_yt(NU - 2)
            copy_logits(B - 2)
            copy_yt(NU - 1)
            router_exps(B - 2)
            copy_xn2(B - 1)
            copy_logits(B - 1)
            router_exps(B - 1)

            def count(g):
                act.wait_ge(spread_ps, HT * (g + 1))
                if g:
                    act.wait_ge(count_act, g)
                act.activation(junk[:, 1, :], rank_bank(g, 1), ACT.Sign, bias=slot_c[:, 1:2], scale=-1.0,
                               accum_out=cnt[:, 1, g:g + 1]).then_inc(count_act, 1)

            act.wait_ge(cum_ps, HT)
            act.activation(cumc[:, 512:1024], bank(1)[0:E, :], ACT.Copy).then_inc(cumc_act, 1)
            act.wait_ge(slotc_ready, 1)
            for g in range(AHEAD):
                count(g)

            for g in range(NG):
                act.wait_ge(up_ps, g + 1)
                if g:
                    act.wait_ge(hh_ready, g)
                act.activation(sil[:, :], up_bank[:, 0:F], ACT.Silu).then_inc(sil_ready, 1)
                act.wait_ge(ht_ps, g + 1)
                if g >= 2:
                    act.wait_ge(down_ps, g - 1)
                act.activation(ht[:, g % 2, :], down_bank[0:F, 0:P], ACT.Copy).then_inc(ht_ready, 1)
                if g + AHEAD < NG:
                    act.wait_ge(spread_ps, HT * (g + AHEAD + 1))
                    act.wait_ge(count_act, g + AHEAD)
                    act.activation(junk[:, :, :].rearrange("p h t -> p (h t)"), ps[3][:, :], ACT.Sign,
                                   bias=slot_c[:, 1:2], scale=-1.0,
                                   accum_out=cnt[:, 1, g + AHEAD:g + AHEAD + 1]).then_inc(count_act, 1)
                act.wait_ge(down_ps, g + 1)
                act.wait_ge(gate_ready, g + 1)
                if g >= 2:
                    act.wait_ge(comb_ps, g - 1)
                act.activation(y3[:, g % 2, 0, :], down_bank[:, 0:C], ACT.Copy,
                               scale=gate[:, g:g + 1]).then_inc(yh_ready, 1)

        @block.tensor
        def _(pe):
            def transpose_x(b):
                pe.wait_ge(xn_ready, HT * (b + 1))
                if b == 0:
                    pe.wait_ge(id_ready, 1)
                if b >= 2:
                    pe.wait_ge(xt_ready, b - 1)
                for t in range(HT):
                    for k in range(KC):
                        mm = pe.transpose(bank(b % 2)[:, k * T + t * P:k * T + (t + 1) * P],
                                          xn[:, b, t, k * P:(k + 1) * P], id32[:, :])
                mm.then_inc(xt_ps, 1)

            def qk(b):
                pe.wait_ge(xt_ready, b + 1)
                if b == 0:
                    pe.wait_ge(scaled, 2)
                if b >= 2:
                    pe.wait_ge(r_ready, 4 * (b - 1))
                for m in range(4):
                    for k in range(KC):
                        mm = pe.matmul(ps[1 + b % 2][:, m * T:(m + 1) * T], w_qk[:, k, m * P:(m + 1) * P],
                                       xnt[:, b % 2, k, :], start=(k == 0), stop=(k == KC - 1))
                mm.then_inc(qk_ps, 1)

            def v(b):
                if b == 0:
                    pe.wait_ge(wv_in, 16)
                if b >= 2:
                    pe.wait_ge(v_ready, HT * (b - 1))
                for t in range(HT):
                    for k in range(KC):
                        mm = pe.matmul(bank(6 + b % 2)[:, t * C:(t + 1) * C], xnt[:, b % 2, k, t * P:(t + 1) * P],
                                       w_v[:, k, :], start=(k == 0), stop=(k == KC - 1))
                mm.then_inc(v_ps, 1)

            def keep_clock(n, unused):
                for _ in range(n):
                    pe.matmul(bank(unused), ones[:, 0:P], ones[:, :], start=True, stop=True)

            pe.wait_ge(ones_ready, 1)
            keep_clock(WARM_UP, 7)
            transpose_x(0)
            for b in range(B):
                qk(b)
                if b + 1 < B:
                    transpose_x(b + 1)
                v(b)

            def scores(u, p):
                b, g, n = u // 2, u % 2, PIECES * u + p
                if n == 0:
                    pe.wait_ge(attn_const, ATTN_CONSTS)
                    pe.wait_ge(xt_ready, B)
                if p == 0 and g == 0:
                    pe.wait_ge(packed[b], 16 * N_PACK)
                if n >= 2:
                    pe.wait_ge(max_done, n - 1)
                nh, w, qt = (4, P, 0) if p < 2 else (2, T, 1)
                h0 = 4 * p if p < 2 else 2 * (p - 2)
                o = bank(p % 2).rearrange("q (h k) -> q h k", k=w)
                pe.matmul(o[:, :, w - P:w], id16[:, :], causal[:, :].unsqueeze(1).to_broadcast([P, nh, P]),
                          start=True, stop=False, skip_group_check=True)
                for h in range(nh):
                    mm = pe.matmul(o[:, h, :], q_of(b, g, h0 + h, qt * P, (qt + 1) * P, KP),
                                   k_of(b, g, h0 + h, 0, w, KP), start=False, stop=(h == nh - 1),
                                   skip_group_check=True)
                mm.then_inc(s_ps, 1)

            def negmax(u):
                pe.wait_ge(nmp_ready, u + 1)
                misc_wait("negmax", u)
                o = misc[0:2 * HG, 0:P].bitcast(BF16)
                for t in range(HT):
                    mm = pe.transpose(o[:, t * P:(t + 1) * P],
                                      nmp[:, u % 2, t, :, :].rearrange("p a h -> p (a h)"), id16[:, :])
                mm.then_inc(misc_ps, 1)

            def misc_wait(kind, n):
                if MISC[kind, n]:
                    pe.wait_ge(misc_free, MISC[kind, n])
                else:
                    pe.wait_ge(v_ready, HT * B)

            def scores_t(u, j):
                b, g, n = u // 2, u % 2, STP * u + j
                if j == 0:
                    pe.wait_ge(negrow_in[u % 2], 16 * (u // 2 + 1))
                if n == 0:
                    pe.wait_ge(r_ready, 4 * B)
                    pe.wait_ge(h_ready, 4 * B)
                if n >= 2:
                    pe.wait_ge(exp_done, n - 1)
                o = ps[1 + n % 2]
                if j < 2:
                    for h in range(4):
                        mm = pe.matmul(o[:, h * T:(h + 1) * T], k_of(b, g, 4 * j + h, 0, P, KP + 2),
                                       q_of(b, g, 4 * j + h, 0, T, KP + 2), start=True, stop=True)
                else:
                    for h in range(HG):
                        mm = pe.matmul(o[:, h * P:(h + 1) * P], k_of(b, g, h, P, T, KP + 2),
                                       q_of(b, g, h, P, T, KP + 2), start=True, stop=True)
                mm.then_inc(st_ps, 1)

            def pv(u):
                b, g = u // 2, u % 2
                pe.wait_ge(causal_done, STP * (u + 1))
                if u == 0:
                    pe.wait_ge(v_ready, HT * B)
                    pe.wait_ge(v_ones, B)
                elif u == NU - 1:
                    pe.wait_ge(max_done, PIECES * NU)
                else:
                    pe.wait_ge(yt_ready, u)
                for half in range(2):
                    for kt in range(HT):
                        for q in range(4):
                            h = 4 * half + q
                            buf = STP * u + (half if kt == 0 else 2)
                            n = T if kt == 0 else P
                            c0 = (q if kt == 0 else h) * n
                            mm = pe.matmul(pv_bank(u)[32 * q:32 * q + 32, half * T + kt * P:(half + 1) * T],
                                           vz[:, kt * B + b, HG * g + h, :], pt[:, buf % (2 * STP), c0:c0 + n],
                                           start=(half == 0 and kt == 0), stop=(half == 1 and kt == 1),
                                           skip_group_check=True)
                mm.then_inc(pv_ps, 1)

            def queries_on_partitions(u):
                pe.wait_ge(yv_ready, u + 1)
                for t in range(HT):
                    for half in range(2):
                        mm = pe.transpose(pv_bank(u)[:, t * T + half * P:t * T + (half + 1) * P],
                                          yv[:, half, t * P:(t + 1) * P], id32[:, :])
                mm.then_inc(yv_ps, 1)

            def dims_on_partitions(u):
                pe.wait_ge(yn_ready, u + 1)
                for t in range(HT):
                    mm = pe.transpose(pv_bank(u)[:, t * P:(t + 1) * P],
                                      yn[:, t * HG:(t + 1) * HG, :].rearrange("p h d -> p (h d)"), id32[:, :])
                mm.then_inc(yt_ps, 1)

            def project(b, t):
                if t == 0:
                    pe.wait_ge(yt_ready, 2 * b + 2)
                    misc_wait("proj", b)
                for k in range(KC):
                    mm = pe.matmul(misc[:, t * C:(t + 1) * C], y_t[:, b % 2, k, t * P:(t + 1) * P],
                                   w_proj[:, k, :], start=(k == 0), stop=(k == KC - 1))
                if t == HT - 1:
                    mm.then_inc(misc_ps, 1)

            def transpose_xn2(b):
                pe.wait_ge(xn2_ready, HT * (b + 1))
                misc_wait("xt", b)
                for t in range(HT):
                    for k in range(KC):
                        mm = pe.transpose(misc[:, k * T + t * P:k * T + (t + 1) * P],
                                          rows[:, t * B + b, k * P:(k + 1) * P], id32[:, :])
                mm.then_inc(misc_ps, 1)

            def logits(b):
                misc_wait("logits", b)
                for t in range(HT):
                    for k in range(KC):
                        mm = pe.matmul(misc[:, t * E:(t + 1) * E], xt2[:, k, t * P:(t + 1) * P], w_rt[:, k, :],
                                       start=(k == 0), stop=(k == KC - 1))
                mm.then_inc(misc_ps, 1)

            def ranks(b):
                pe.wait_ge(sel_ready, b + 1)
                if b == 0:
                    pe.wait_ge(moe_const, MOE_CONSTS)
                    pe.wait_ge(max_done, PIECES * NU)
                    pe.wait_ge(yt_ready, NU)
                in_order = before[:, 3 - b:7 - b, :].rearrange("p a t -> p (a t)")
                for half, tile, r in [(0, b, in_order), (1, b, ones[:, :]), (1, B + b, in_order)]:
                    mm = pe.matmul(bank(half)[0:E, :], sel[:, tile, :], r, start=(b == 0 and tile == b),
                                   stop=(b == B - 1 and r is in_order))
                    if b == B - 1 and r is in_order:
                        mm.then_inc(cum_ps, 1)

            for s in range(NU):
                router, proj = BATCH["router"](s), BATCH["project"](s)
                for p in range(EARLY.get(s - 1, 0), 2):
                    scores(s, p)
                if s:
                    negmax(s - 1)
                if s == 2:
                    scores_t(0, 0)
                if s >= 3:
                    queries_on_partitions(s - 3)
                if s >= 2:
                    scores_t(s - 2, 1)
                scores(s, 2)
                if s >= 2:
                    scores_t(s - 2, 2)
                if s >= 3:
                    dims_on_partitions(s - 3)
                scores(s, 3)
                if router is not None:
                    transpose_xn2(router)
                scores(s, 4)
                if proj is not None:
                    project(proj, 0)
                if s > 1 and proj is None:
                    scores_t(s - 1, 0)
                scores(s, 5)
                if proj is not None:
                    project(proj, 1)
                    scores_t(s - 1, 0)
                if router is not None:
                    logits(router)
                if s == NU - 1:
                    negmax(NU - 1)
                for p in range(EARLY.get(s, 0)):
                    scores(s + 1, p)
                if s >= 2:
                    pv(s - 2)
            scores_t(NU - 2, 1)
            queries_on_partitions(NU - 3)
            scores_t(NU - 2, 2)
            dims_on_partitions(NU - 3)
            scores_t(NU - 1, 0)
            scores_t(NU - 1, 1)
            project(B - 2, 0)
            scores_t(NU - 1, 2)
            project(B - 2, 1)
            pv(NU - 2)
            pe.wait_ge(max_done, PIECES * NU)
            pv(NU - 1)
            queries_on_partitions(NU - 2)
            transpose_xn2(B - 2)
            queries_on_partitions(NU - 1)
            dims_on_partitions(NU - 2)
            logits(B - 2)
            dims_on_partitions(NU - 1)
            project(B - 1, 0)
            project(B - 1, 1)
            for b in range(B - 1):
                ranks(b)
            pe.wait_ge(exp_done, STP * NU)
            keep_clock(6, 4)
            transpose_xn2(B - 1)
            keep_clock(4, 4)
            logits(B - 1)
            keep_clock(7, 4)
            ranks(B - 1)
            keep_clock(4, 4)

            def spread_ranks(g):
                if AHEAD > g >= 2:
                    pe.wait_ge(count_dve, g - 1)
                    pe.wait_ge(count_act, g - 1)
                elif g >= AHEAD:
                    pe.wait_ge(count_act, g)
                for half in range(HT):
                    pe.matmul(rank_bank(g, half), spread[:, g, :], cumc[:, half * 512:(half + 1) * 512],
                              start=True, stop=True).then_inc(spread_ps, 1)

            pe.wait_ge(cumc_dve, 1)
            pe.wait_ge(cumc_act, 1)
            pe.wait_ge(misc_free, len(MISC))
            for g in range(AHEAD):
                spread_ranks(g)

            def transpose_rows(g):
                pe.wait_ge(row_in[g % 4], 16 * (g // 4 + 1))
                if g:
                    pe.wait_ge(hh_ready, g)
                for k in range(KC):
                    mm = pe.transpose(up_bank[:, k * P:(k + 1) * P], grow[:, g % 4, k * P:(k + 1) * P], id32[:, :])
                mm.then_inc(xg_ps, 1)

            def part(g, n, tiles):
                for t in tiles:
                    mm = pe.matmul(bank(t // 2)[:, (t % 2) * C:(t % 2 + 1) * C], onehot[:, g % 2, t * P:(t + 1) * P],
                                   y3[:, g % 2, n, :], start=False, stop=(g == NG - 1 and n == 2),
                                   skip_group_check=True)
                    if n == 2 and t < ALWAYS and (t == tiles[-1] or g == NG - 1):
                        mm.then_inc(comb_ps, 1)

            def combine(g, n):
                if n == 0:
                    pe.wait_ge(hot_ready, g + 1)
                    pe.wait_ge(yh_ready, g + 1)
                elif n == 1:
                    pe.wait_ge(ym_ready, g + 1)
                else:
                    pe.wait_ge(yl_ready, g + 1)
                    word, place = reach[g // (NG // 2)], 4 ** (g % (NG // 2))
                    with pe.If((word & 3 * place) > 0):
                        for m in range(3):
                            part(g, m, range(ALWAYS, MORE))
                        with pe.If((word & 2 * place) > 0):
                            for m in range(3):
                                part(g, m, range(MORE, NT))
                part(g, n, range(ALWAYS) if g < NG - 1 else [*range(2, ALWAYS), 0, 1])

            pe.wait_ge(need_ready, 1)
            pe.transpose(bank(0)[0:1, 0:E], need[:, :], id32[0:E, 0:E]).then_inc(need_ps, 1)
            keep_clock(4, 4)
            pe.wait_ge(count_dve, AHEAD)
            pe.wait_ge(count_act, AHEAD)
            pe.wait_ge(zero_ready, 1)
            for n in (2, 3, 1):
                pe.matmul(bank(n), zero16[:, :], ones[:, :], start=True, stop=False, skip_group_check=True)
            keep_clock(2, 4)
            transpose_rows(0)
            for g in range(NG + 1):
                if g < NG:
                    pe.wait_ge(xg_ready, g + 1)
                    pe.wait_ge(w13_in[g], 16)
                    for k in range(KC):
                        for q in range(EG):
                            mm = pe.matmul(up_bank[q * CAP:(q + 1) * CAP, 0:2 * F],
                                           xgt[:, g % 2, k, q * CAP:(q + 1) * CAP], w13_sb[g][:, q, k, :],
                                           start=(k == 0), stop=(k == KC - 1))
                    mm.then_inc(up_ps, 1)
                    if g + AHEAD < NG:
                        spread_ranks(g + AHEAD)
                if g:
                    combine(g - 1, 0)
                if g < NG:
                    pe.wait_ge(hh_ready, g + 1)
                    if g:
                        pe.wait_ge(yr_ready, g)
                    pe.transpose(down_bank[0:F, 0:P], hh[:, :], id32[:, :]).then_inc(ht_ps, 1)
                if g:
                    combine(g - 1, 1)
                if g + 1 < NG:
                    transpose_rows(g + 1)
                if g < NG:
                    pe.wait_ge(ht_ready, g + 1)
                    pe.wait_ge(w2_in[g], 16)
                    for q in range(EG):
                        mm = pe.matmul(down_bank[q * CAP:(q + 1) * CAP, 0:C], ht[:, g % 2, q * CAP:(q + 1) * CAP],
                                       w2_sb[g % W2S][:, q, :], start=True, stop=True)
                    mm.then_inc(down_ps, 1)
                if g == 0:
                    pe.wait_ge(need_in, 1)
                    pe.matmul(bank(0), zero16[:, :], ones[:, :], start=True, stop=False, skip_group_check=True)
                    reach = [pe.value_load(reach_i[0:1, w:w + 1]) for w in range(2)]
                if g:
                    combine(g - 1, 2)

        @block.vector
        def _(dve):
            steps = [0]

            def link(ins):
                steps[0] += 1
                ins.then_inc(dve_step, 1)
                dve.wait_ge(dve_step, steps[0])

            def moments(b):
                for t in range(HT):
                    ins = dve.bn_stats(stats[:, b, t, :], x_sb[:, t * B + b, :])
                    if t == HT - 1:
                        link(ins)
                for t in range(HT):
                    ins = dve.bn_aggr(mv[:, b, t, :], stats[:, b, t, :])
                    if t == HT - 1:
                        link(ins)
                return dve.tensor_scalar(ve[:, b, :], mv[:, b, :, 1], EPS, None, ALU.add)

            def moments1(b):
                dve.wait_ge(x_in[b], 16)
                moments(b).then_inc(var_ready, 1)

            def norm1(b):
                dve.wait_ge(rstd_ready, b + 1)
                for t in range(HT):
                    dve.tensor_scalar(xn[:, b, t, :], x_sb[:, t * B + b, :], mv[:, b, t, 0:1],
                                      rstd[:, b, t:t + 1], ALU.subtract, ALU.mult).then_inc(xn_ready, 1)

            dve.memset(ones[:, :], 1.0).then_inc(ones_ready, 1)
            moments1(0)
            dve.wait_ge(wqk_in, 16)
            dve.wait_ge(bqk_in, 16)
            dve.tensor_scalar(w_qk[:, :, 0:C], w_qk[:, :, 0:C], SCALE, None, ALU.mult).then_inc(scaled, 1)
            dve.tensor_scalar(b_qk[:, 0:2], b_qk[:, 0:2], SCALE, None, ALU.mult).then_inc(scaled, 1)
            norm1(0)
            moments1(1)
            moments1(2)
            norm1(1)
            norm1(2)
            for b in range(B):
                if b >= 2:
                    dve.wait_ge(l_ready, b - 1)
                for m in range(4):
                    dve.wait_ge(h_ready, 4 * b + 2 * (m // 2) + 2)
                    dve.scalar_tensor_tensor(out=res[:, b % 2, m, :], in0=ps[1 + b % 2][:, m * T:(m + 1) * T],
                                             scalar=b_qk[:, m:m + 1],
                                             in1=spl[:, b % 2, m // 2, (m % 2) * T:(m % 2 + 1) * T],
                                             op0=ALU.add, op1=ALU.subtract).then_inc(r_ready, 1)
                dve.wait_ge(v_ps, b + 1)
                if b == 0:
                    dve.wait_ge(small_in, N_SMALL)
                for t in range(HT):
                    dve.tensor_tensor(vz[:, t * B + b, :, 0:D],
                                      bank(6 + b % 2)[:, t * C:(t + 1) * C].rearrange("p (h d) -> p h d", d=D),
                                      b_v[:, :].rearrange("p (h d) -> p h d", d=D), ALU.add).then_inc(v_ready, 1)
                if b == 0:
                    moments1(3)
                    norm1(3)

            def row_max(u, p):
                n = PIECES * u + p
                dve.wait_ge(s_ps, n + 1)
                w, qt = (P, 0) if p < 2 else (T, 1)
                h0, nh = (4 * p, 4) if p < 2 else (2 * (p - 2), 2)
                dve.tensor_reduce(nm[:, u % 2, qt, h0:h0 + nh], bank(p % 2).rearrange("q (h k) -> q h k", k=w),
                                  AX.X, ALU.max, negate=True).then_inc(max_done, 1)

            def negmax_parts(u):
                dve.wait_ge(max_done, PIECES * (u + 1))
                if u >= 2:
                    dve.wait_ge(misc_ps, MISC["negmax", u - 2] + 1)
                link(dve.tensor_copy(nmp[:, u % 2, :, 0, :], nm[:, u % 2, :, :]))
                dve.tensor_tensor(nmp[:, u % 2, :, 1, :], nm[:, u % 2, :, :], nmp[:, u % 2, :, 0, :],
                                  ALU.subtract).then_inc(nmp_ready, 1)

            def over_sums(u):
                dve.wait_ge(yv_ps, u + 1)
                if u == NU - 1:
                    dve.wait_ge(yt_ps, u)
                y = pv_bank(u).rearrange("p (h a) -> p h a", a=2 * D)
                link(dve.reciprocal(rden[:, :].unsqueeze(2), y[:, :, D:D + 1]))
                dve.tensor_tensor(yn[:, :, :], y[:, :, 0:D], rden[:, :].unsqueeze(2).to_broadcast([P, HT * HG, D]),
                                  ALU.mult).then_inc(yn_ready, 1)

            def residual(b):
                dve.wait_ge(misc_ps, MISC["proj", b] + 1)
                dve.wait_ge(xb_ready, HT * (b + 1))
                dve.tensor_tensor(x_sb[:, b::B, :], misc.rearrange("p (t c) -> p t c", t=HT), x_sb[:, b::B, :],
                                  ALU.add).then_inc(misc_free, 1)
                dve.wait_ge(misc_free, MISC["proj", b] + 1)
                moments(b).then_inc(var2_ready, 1)

            def norm2(b):
                dve.wait_ge(rstd2_ready, b + 1)
                for t in range(HT):
                    dve.tensor_scalar(rows[:, t * B + b, 0:C], x_sb[:, t * B + b, :], mv[:, b, t, 0:1],
                                      rstd[:, b, t:t + 1], ALU.subtract, ALU.mult).then_inc(xn2_ready, 1)

            def choose(b):
                dve.wait_ge(misc_free, MISC["logits", b] + 1)
                if b:
                    dve.wait_ge(e_ready, 2 * HT * b)
                dve.max(m8[:, 0, :], lg[:, 0, :])
                link(dve.max(m8[:, 1, :], lg[:, 1, :]))
                dve.tensor_scalar(negm[:, :], m8[:, :, 0], -1.0, None, ALU.mult).then_inc(negm_ready, 1)
                dve.match_replace(lr[:, 0, :], m8[:, 0, :], lg[:, 0, :], -3.0e38)
                link(dve.match_replace(lr[:, 1, :], m8[:, 1, :], lg[:, 1, :], -3.0e38))
                dve.tensor_tensor(sel[:, b::B, :], lr[:, :, :], lg[:, :, :], ALU.not_equal).then_inc(sel_ready, 1)

            def expert_weights(b):
                dve.wait_ge(e_ready, 2 * HT * (b + 1))
                dve.wait_ge(sel_ready, b + 1)
                link(dve.reciprocal(wrec[:, :], wsum[:, :]))
                for t in range(HT):
                    dve.scalar_tensor_tensor(out=rows[:, t * B + b, C:ROW], in0=ee[:, t, :], scalar=wrec[:, t:t + 1],
                                             in1=sel[:, t * B + b, :], op0=ALU.mult,
                                             op1=ALU.mult).then_inc(rows_ready, 1)

            for s in range(NU):
                router, proj, weights = BATCH["router"](s), BATCH["project"](s), BATCH["weights"](s)
                row_max(s, 0)
                row_max(s, 1)
                if s >= 3:
                    over_sums(s - 3)
                if router is not None:
                    norm2(router)
                for p in range(2, PIECES):
                    row_max(s, p)
                    if p == 3 and weights is not None:
                        expert_weights(weights)
                negmax_parts(s)
                if proj is not None:
                    residual(proj)
                if router is not None:
                    choose(router)
            over_sums(NU - 3)
            residual(B - 2)
            expert_weights(B - 3)
            norm2(B - 2)
            over_sums(NU - 2)
            dve.wait_ge(moe_const, MOE_CONSTS)
            link(dve.tensor_reduce(slot_c[:, 0:1], pc[:, :], AX.X, ALU.add))
            dve.tensor_scalar(slot_c[:, 1:2], slot_c[:, 0:1], 0.5, None, ALU.add).then_inc(slotc_ready, 1)
            over_sums(NU - 1)
            choose(B - 2)
            expert_weights(B - 2)
            residual(B - 1)
            norm2(B - 1)
            choose(B - 1)

            def count(g):
                dve.wait_ge(spread_ps, HT * g + 1)
                if g:
                    dve.wait_ge(count_dve, g)
                dve.tensor_scalar(junk[:, 0, :], rank_bank(g, 0), slot_c[:, 0:1], 0.0, ALU.is_le, ALU.add,
                                  accum_out=cnt[:, 0, g:g + 1]).then_inc(count_dve, 1)

            def tokens(g):
                dve.wait_ge(count_act, g + 2)
                dve.wait_ge(count_dve, g + 2)
                both = cnt[:, 0, g:g + 2]
                link(dve.scalar_tensor_tensor(out=both, in0=cnt[:, 1, g:g + 2], scalar=0.5, in1=both,
                                              op0=ALU.mult, op1=ALU.add))
                dve.tensor_scalar(tok_i[:, g:g + 2], both, NTOK / 4, NTOK - 1.0, ALU.add, ALU.min)\
                    .then_inc(tok_ready, 1)
                dve.tensor_scalar(tok_n[:, g:g + 2], both, NTOK / 4, None, ALU.add).then_inc(tokn_ready, 1)

            def token_tiles_needed():
                dve.wait_ge(cumc_act, 1)
                dve.wait_ge(cumc_dve, 1)
                ends = cumc[:, :].rearrange("e (h b j s) -> e h b j s", h=HT, b=B, s=TS)[:, :, B - 1, :, TS - 1]
                dve.tensor_scalar(need_at[:, :].rearrange("e (h j) -> e h j", h=HT), ends, float(CAP), 0.0,
                                  ALU.is_lt, ALU.add, accum_out=need[:, :]).then_inc(need_ready, 1)

            def reach_of_slot_tiles():
                dve.wait_ge(need_ps, 1)
                link(dve.tensor_reduce(past[:, 0, :, :], bank(0)[0:1, 0:E].rearrange("p (w g q) -> p w g q", w=2, q=EG),
                                       AX.X, ALU.max))
                link(dve.scalar_tensor_tensor(out=past[:, 1, :, :], in0=past[:, 0, :, :], scalar=float(MORE), in1=digit[:, :, :],
                                              op0=ALU.is_ge, op1=ALU.mult))
                link(dve.scalar_tensor_tensor(out=past[:, 0, :, :], in0=past[:, 0, :, :], scalar=float(ALWAYS), in1=digit[:, :, :],
                                              op0=ALU.is_ge, op1=ALU.mult))
                link(dve.tensor_tensor(past[:, 0, :, :], past[:, 0, :, :], past[:, 1, :, :], ALU.add))
                link(dve.tensor_reduce(reach_f[:, :], past[:, 0, :, :], AX.X, ALU.add))
                dve.tensor_scalar(reach_i[:, :], reach_f[:, :], 0.0, None, ALU.add).then_inc(need_in, 1)

            dve.wait_ge(cum_ps, 1)
            dve.tensor_scalar(cumc[:, 0:512], bank(0)[0:E, :], 2.0 * CAP, None, ALU.min).then_inc(cumc_dve, 1)
            expert_weights(B - 1)
            for g in range(AHEAD):
                count(g)
                if g % 2:
                    tokens(g - 1)
                if g == 1:
                    token_tiles_needed()
            reach_of_slot_tiles()

            def take_rows(g):
                dve.wait_ge(row_in[g % 4], 16 * (g // 4 + 1))
                link(dve.tensor_tensor(g4[:, :], grow[:, g % 4, C + EG * g:C + EG * (g + 1)], eq4[:, :], ALU.mult))
                dve.tensor_reduce(gate[:, g:g + 1], g4[:, :], AX.X, ALU.add).then_inc(gate_ready, 1)
                dve.wait_ge(xg_ps, g + 1)
                if g >= 2:
                    dve.wait_ge(up_ps, g - 1)
                dve.tensor_copy(xgt[:, g % 2, :, :].rearrange("p k t -> p (k t)"), up_bank[:, 0:KC * P])\
                    .then_inc(xg_ready, 1)

            def third_part(g):
                dve.wait_ge(ym_ready, g + 1)
                dve.tensor_tensor(y3[:, g % 2, 2, :], yr[:, :], y3[:, g % 2, 1, :], ALU.subtract)\
                    .then_inc(yl_ready, 1)

            take_rows(0)
            for g in range(NG):
                dve.wait_ge(sil_ready, g + 1)
                if g:
                    dve.wait_ge(ht_ps, g)
                dve.tensor_tensor(hh[:, :], up_bank[:, F:2 * F], sil[:, :], ALU.mult).then_inc(hh_ready, 1)
                if g:
                    third_part(g - 1)
                dve.wait_ge(tokn_ready, g // 2 + 1)
                if g >= 2:
                    dve.wait_ge(comb_ps, g - 1)
                dve.tensor_scalar(onehot[:, g % 2, :], tokid[:, :], tok_n[:, g:g + 1], None, ALU.is_equal)\
                    .then_inc(hot_ready, 1)
                if g + 1 < NG:
                    take_rows(g + 1)
                dve.wait_ge(yh_ready, g + 1)
                if g:
                    dve.wait_ge(yl_ready, g)
                dve.scalar_tensor_tensor(out=yr[:, :], in0=down_bank[:, 0:C], scalar=gate[:, g:g + 1],
                                         in1=y3[:, g % 2, 0, :], op0=ALU.mult, op1=ALU.subtract)\
                    .then_inc(yr_ready, 1)
                dve.wait_ge(yr_ready, g + 1)
                dve.tensor_copy(y3[:, g % 2, 1, :], yr[:, :]).then_inc(ym_ready, 1)
            third_part(NG - 1)
            dve.wait_ge(x_tok_in, 16 * NT * B)
            for pair in FINISH:
                dve.wait_ge(comb_ps, NG + 2 if pair == 0 else NG)
                dve.tensor_tensor(x_tok[:, 2 * pair:2 * pair + 2, :], bank(pair).rearrange("p (t c) -> p t c", t=2),
                                  x_tok[:, 2 * pair:2 * pair + 2, :], ALU.add).then_inc(fin_ready, 1)


_INS = ["x", "wqk", "bqk", "wv", "bv", "wproj", "bproj", "rwt", "w13", "w2"]


def kernel(L0_attn_x, L0_attn_w_attn, L0_attn_b_attn, L0_attn_w_proj, L0_attn_b_proj, L0_ffn_router_w, L0_ffn_w1,
           L0_ffn_v1, L0_ffn_w2):
    import numpy as np
    import concourse.bacc as bacc
    from concourse.bass_utils import run_bass_kernel_spmd

    def a(v):
        return np.ascontiguousarray(v)

    qk = np.asarray(L0_attn_w_attn)[:, :2 * C].reshape(C, 2, 2, HG, D).transpose(0, 1, 2, 4, 3).reshape(C, 2 * C)
    bqk = np.asarray(L0_attn_b_attn)[:2 * C].reshape(4, HG, D).transpose(2, 1, 0).reshape(P, 4)
    w1 = np.asarray(L0_ffn_w1).reshape(NG, EG, F, KC, P)
    v1 = np.asarray(L0_ffn_v1).reshape(NG, EG, F, KC, P)
    w13 = np.concatenate([w1, v1], axis=2).transpose(0, 4, 1, 3, 2)
    w2 = np.asarray(L0_ffn_w2).reshape(NG, EG, F, C).transpose(0, 2, 1, 3)
    host = {
        "x": a(L0_attn_x), "wqk": a(qk), "bqk": a(bqk), "wv": a(np.asarray(L0_attn_w_attn)[:, 2 * C:]),
        "bv": a(np.asarray(L0_attn_b_attn)[2 * C:]), "wproj": a(L0_attn_w_proj), "bproj": a(L0_attn_b_proj),
        "rwt": a(np.asarray(L0_ffn_router_w).T), "w13": a(w13), "w2": a(w2),
    }
    nc = bacc.Bacc("TRN2", target_bir_lowering=False, num_devices=1)
    args = [nc.dram_tensor(f"in_{n}", host[n].shape, mybir.dt.from_np(host[n].dtype), kind="ExternalInput").ap()
            for n in _INS]
    out = nc.dram_tensor("out_0", (B, T, C), F32, kind="ExternalOutput").ap()
    build(nc, *args, out)
    r = run_bass_kernel_spmd(nc, [{f"in_{n}": host[n] for n in _INS}], core_ids=[0])
    return r.results[0]["out_0"]
```
